# Optimizing a Trainium2 kernel written in Bass

```python
import numpy as np
import jax
import jax.numpy as jnp

def _softmax(x, axis=-1):
    return jax.nn.softmax(x, axis=axis)

def _gelu(x):
    return jax.nn.gelu(x, approximate=True)

def _silu(x):
    return jax.nn.silu(x)

def _sigmoid(x):
    return jax.nn.sigmoid(x)

def _layernorm(x, axis=-1, eps=1e-05):
    m = jnp.mean(x, axis=axis, keepdims=True)
    v = jnp.var(x, axis=axis, keepdims=True)
    return (x - m) / jnp.sqrt(v + eps)

def _scatter_add(tgt, idx, src, axis=0):
    return tgt.at[idx].add(src)

def _segment_sum(src, seg, n):
    return jax.ops.segment_sum(src, seg, n)
kernel_name = 'mk_seq_postln_d1_jaxref_r8_bf8b39'

def setup_inputs(seed: int=0):
    np.random.seed(seed)
    _w = jnp.asarray

    def _L0_attn_setup():
        import jax, jax.numpy as jnp
        import numpy as np
        from functools import partial
        LN_EPS = 1000000.0
        FEAT_EPS = 1e-06

        def _layernorm(x, gamma, beta):
            mu = jnp.mean(x, axis=-1, keepdims=True)
            var = jnp.var(x, axis=-1, keepdims=True)
            return gamma * (x - mu) / jnp.sqrt(var + LN_EPS) + beta

        def _phi(x, omega):
            m = omega.shape[0]
            proj = jnp.einsum('bhsd,md->bhsm', x, omega)
            z = proj - 0.5 * jnp.sum(x * x, axis=-1, keepdims=True)
            z = z - jnp.max(z, axis=-1, keepdims=True)
            return jnp.exp(z) / jnp.sqrt(jnp.asarray(m, x.dtype)) + FEAT_EPS

        def _forward(batch, Wq, Wk, Wv, Wo, omega, W1, b1, W2, b2, gamma, beta):
            B, S, D = batch.shape
            M, dh = omega.shape
            H = D // dh
            scale = dh ** (-0.25)

            def heads(W):
                return (batch @ W).reshape(B, S, H, dh).transpose(0, 2, 1, 3)
            q = heads(Wq) * scale
            k = heads(Wk) * scale
            v = heads(Wv)
            qp = _phi(q, omega)
            kp = _phi(k, omega)
            qs = qp.transpose(2, 0, 1, 3)
            ks = kp.transpose(2, 0, 1, 3)
            vs = v.transpose(2, 0, 1, 3)

            def step(carry, qkv):
                S_kv, s_k = carry
                qt, kt, vt = qkv
                S_kv = S_kv + kt[..., :, None] * vt[..., None, :]
                s_k = s_k + kt
                num = jnp.einsum('bhm,bhmd->bhd', qt, S_kv)
                den = jnp.einsum('bhm,bhm->bh', qt, s_k)
                return ((S_kv, s_k), num / (den[..., None] + FEAT_EPS))
            carry0 = (jnp.zeros((B, H, M, dh), batch.dtype), jnp.zeros((B, H, M), batch.dtype))
            _, outs = jax.lax.scan(step, carry0, (qs, ks, vs))
            attn = outs.transpose(1, 0, 2, 3).reshape(B, S, D) @ Wo
            h = _layernorm(batch + attn, gamma, beta)
            out = jnp.maximum(h @ W1 + b1, 0.0) @ W2 + b2
            return out
        key = jax.random.key(seed)
        ks = jax.random.split(key, 8)
        B, S, D, H, dh, M, DFF = (4, 128, 128, 16, 64, 128, 512)
        w = 0.02
        return {'batch': jax.random.normal(ks[0], (B, S, D), jnp.float32), 'Wq': jax.random.normal(ks[1], (D, D), jnp.float32) * w, 'Wk': jax.random.normal(ks[2], (D, D), jnp.float32) * w, 'Wv': jax.random.normal(ks[3], (D, D), jnp.float32) * w, 'Wo': jax.random.normal(ks[4], (D, D), jnp.float32) * w, 'omega': jax.random.normal(ks[5], (M, dh), jnp.float32), 'W1': jax.random.normal(ks[6], (D, DFF), jnp.float32) * w, 'b1': jnp.zeros((DFF,), jnp.float32), 'W2': jax.random.normal(ks[7], (DFF, D), jnp.float32) * w, 'b2': jnp.zeros((D,), jnp.float32), 'gamma': jnp.ones((D,), jnp.float32), 'beta': jnp.zeros((D,), jnp.float32)}
    _L0_attn_in = _L0_attn_setup()

    def _L0_ffn_setup():
        import jax, jax.numpy as jnp
        import numpy as np
        import math
        B, S, D = (4, 256, 128)
        E, DFF = (16, 256)
        CAP_FACTOR = 2.0
        ROUTER_HIDDEN = 128
        CAPACITY = int(math.ceil(S * CAP_FACTOR / E))
        key = jax.random.key(seed)
        ks = jax.random.split(key, 6)

        def uinit(k, shape, fan_in):
            bound = math.sqrt(3.0) * math.sqrt(1.0 / 3.0) / math.sqrt(fan_in)
            return jax.random.uniform(k, shape, jnp.float32, -bound, bound)
        return {'hidden_states': jax.random.normal(ks[0], (B, S, D), jnp.float32), 'router_w1': jax.random.normal(ks[1], (D, ROUTER_HIDDEN), jnp.float32) / math.sqrt(D), 'router_w2': jax.random.normal(ks[2], (ROUTER_HIDDEN, E), jnp.float32) / math.sqrt(ROUTER_HIDDEN), 'w1': uinit(ks[3], (E, D, DFF), D), 'w2': uinit(ks[4], (E, D, DFF), D), 'w3': uinit(ks[5], (E, DFF, D), DFF)}
    _L0_ffn_in = _L0_ffn_setup()
    _d = {'L0_attn_batch': _L0_attn_in['batch'], 'L0_attn_Wq': _L0_attn_in['Wq'], 'L0_attn_Wk': _L0_attn_in['Wk'], 'L0_attn_Wv': _L0_attn_in['Wv'], 'L0_attn_Wo': _L0_attn_in['Wo'], 'L0_attn_omega': _L0_attn_in['omega'], 'L0_attn_W1': _L0_attn_in['W1'], 'L0_attn_b1': _L0_attn_in['b1'], 'L0_attn_W2': _L0_attn_in['W2'], 'L0_attn_b2': _L0_attn_in['b2'], 'L0_attn_gamma': _L0_attn_in['gamma'], 'L0_attn_beta': _L0_attn_in['beta'], 'L0_ffn_router_w1': _L0_ffn_in['router_w1'], 'L0_ffn_router_w2': _L0_ffn_in['router_w2'], 'L0_ffn_w1': _L0_ffn_in['w1'], 'L0_ffn_w2': _L0_ffn_in['w2'], 'L0_ffn_w3': _L0_ffn_in['w3']}
    _x0 = _d['L0_attn_batch']
    _d['L0_attn_batch'] = jax.random.normal(jax.random.fold_in(jax.random.key(seed), 1), (16, 256, 128), dtype=_x0.dtype)
    del _x0
    return _d

def reference(L0_attn_batch, L0_attn_Wq, L0_attn_Wk, L0_attn_Wv, L0_attn_Wo, L0_attn_omega, L0_attn_W1, L0_attn_b1, L0_attn_W2, L0_attn_b2, L0_attn_gamma, L0_attn_beta, L0_ffn_router_w1, L0_ffn_router_w2, L0_ffn_w1, L0_ffn_w2, L0_ffn_w3):

    def _L0_attn_ref(batch, Wq, Wk, Wv, Wo, omega, W1, b1, W2, b2, gamma, beta):
        import jax, jax.numpy as jnp
        import numpy as np
        from functools import partial
        LN_EPS = 1000000.0
        FEAT_EPS = 1e-06

        def _layernorm(x, gamma, beta):
            mu = jnp.mean(x, axis=-1, keepdims=True)
            var = jnp.var(x, axis=-1, keepdims=True)
            return gamma * (x - mu) / jnp.sqrt(var + LN_EPS) + beta

        def _phi(x, omega):
            m = omega.shape[0]
            proj = jnp.einsum('bhsd,md->bhsm', x, omega)
            z = proj - 0.5 * jnp.sum(x * x, axis=-1, keepdims=True)
            z = z - jnp.max(z, axis=-1, keepdims=True)
            return jnp.exp(z) / jnp.sqrt(jnp.asarray(m, x.dtype)) + FEAT_EPS

        def _forward(batch, Wq, Wk, Wv, Wo, omega, W1, b1, W2, b2, gamma, beta):
            B, S, D = batch.shape
            M, dh = omega.shape
            H = D // dh
            scale = dh ** (-0.25)

            def heads(W):
                return (batch @ W).reshape(B, S, H, dh).transpose(0, 2, 1, 3)
            q = heads(Wq) * scale
            k = heads(Wk) * scale
            v = heads(Wv)
            qp = _phi(q, omega)
            kp = _phi(k, omega)
            qs = qp.transpose(2, 0, 1, 3)
            ks = kp.transpose(2, 0, 1, 3)
            vs = v.transpose(2, 0, 1, 3)

            def step(carry, qkv):
                S_kv, s_k = carry
                qt, kt, vt = qkv
                S_kv = S_kv + kt[..., :, None] * vt[..., None, :]
                s_k = s_k + kt
                num = jnp.einsum('bhm,bhmd->bhd', qt, S_kv)
                den = jnp.einsum('bhm,bhm->bh', qt, s_k)
                return ((S_kv, s_k), num / (den[..., None] + FEAT_EPS))
            carry0 = (jnp.zeros((B, H, M, dh), batch.dtype), jnp.zeros((B, H, M), batch.dtype))
            _, outs = jax.lax.scan(step, carry0, (qs, ks, vs))
            attn = outs.transpose(1, 0, 2, 3).reshape(B, S, D) @ Wo
            h = _layernorm(batch + attn, gamma, beta)
            out = jnp.maximum(h @ W1 + b1, 0.0) @ W2 + b2
            return out
        return _forward(batch, Wq, Wk, Wv, Wo, omega, W1, b1, W2, b2, gamma, beta)

    def _L0_ffn_ref(hidden_states, router_w1, router_w2, w1, w2, w3):
        import jax, jax.numpy as jnp
        import numpy as np
        import math
        B, S, D = (4, 256, 128)
        E, DFF = (16, 256)
        CAP_FACTOR = 2.0
        ROUTER_HIDDEN = 128
        CAPACITY = int(math.ceil(S * CAP_FACTOR / E))
        b, s, d = hidden_states.shape
        e = w1.shape[0]
        cap = CAPACITY
        router_logits = jax.nn.silu(hidden_states @ router_w1) @ router_w2
        expert_probs = jax.nn.softmax(router_logits.transpose(0, 2, 1), axis=-1)
        expert_weights, token_indices = jax.lax.top_k(expert_probs, cap)
        expert_weights = expert_weights / (expert_weights.sum(-1, keepdims=True) + 1e-09)
        expert_inputs = jax.vmap(lambda h, i: h[i])(hidden_states, token_indices)
        gate = jax.nn.silu(jnp.einsum('becd,edf->becf', expert_inputs, w1))
        value = jnp.einsum('becd,edf->becf', expert_inputs, w2)
        expert_out = jnp.einsum('becf,efd->becd', gate * value, w3)
        weighted = expert_out * expert_weights[..., None]

        def combine(idx, vals):
            return jnp.zeros((s, d), vals.dtype).at[idx.reshape(-1)].add(vals.reshape(-1, d))
        output = jax.vmap(combine)(token_indices, weighted)
        return output
    x = L0_attn_batch
    x = _layernorm(x + _L0_attn_ref(x, L0_attn_Wq, L0_attn_Wk, L0_attn_Wv, L0_attn_Wo, L0_attn_omega, L0_attn_W1, L0_attn_b1, L0_attn_W2, L0_attn_b2, L0_attn_gamma, L0_attn_beta), axis=-1)
    x = _layernorm(x + _L0_ffn_ref(x, L0_ffn_router_w1, L0_ffn_router_w2, L0_ffn_w1, L0_ffn_w2, L0_ffn_w3), axis=-1)
    return x

_drawn_inputs = setup_inputs


def setup_inputs(seed=0):
    import zlib

    import numpy as np

    out = dict(_drawn_inputs(seed))
    spreads = {'L0_attn_b1': (0.0, 0.268),
     'L0_attn_b2': (0.0, 0.1),
     'L0_attn_gamma': (1.0, 0.6),
     'L0_attn_beta': (0.0, 0.8)}
    factors = {'L0_attn_Wq': 64.0,
     'L0_attn_Wk': 64.0,
     'L0_attn_Wv': 64.0,
     'L0_attn_Wo': 64.0,
     'L0_attn_omega': 60.718,
     'L0_attn_W1': 8.0,
     'L0_ffn_router_w1': 8.0,
     'L0_ffn_router_w2': 8.0,
     'L0_ffn_w1': 8.0,
     'L0_ffn_w2': 8.0,
     'L0_ffn_w3': 8.0}
    for name, (base, spread) in spreads.items():
        noise = np.random.default_rng([zlib.crc32(name.encode()), seed]).standard_normal(out[name].shape)
        drawn = base * np.exp(spread * noise) if base else spread * noise
        out[name] = jnp.asarray(drawn.astype(out[name].dtype))
    for name, factor in factors.items():
        out[name] = (out[name] * factor).astype(out[name].dtype)
    return out
```

```python
from contextlib import ExitStack

import concourse.bass as bass
from concourse import mybir

ALU = mybir.AluOpType
ACT = mybir.ActivationFunctionType
AX = mybir.AxisListType
F32 = mybir.dt.float32
F32R = mybir.dt.float32r
BF16 = mybir.dt.bfloat16
I32 = mybir.dt.int32
U32 = mybir.dt.uint32
ds = bass.ds

P = 128
INNER_EPS = 1e6
FEAT_EPS = 1e-6
LN_EPS = 1e-5
WEIGHT_EPS = 1e-9


def post_ln_block(nc, x, Wq, Wk, Wv, Wo, omega, W1, b1, W2, b2, gamma, beta,
                  router_w1, router_w2, w1, w2, w3, logits, out):
    B, S, D = x.shape
    M, DH = omega.shape
    H = D // DH
    FF = W1.shape[1]
    FC = FF // P
    E, _, EF = w1.shape
    EC = EF // P
    HID = router_w1.shape[1]
    T = S // P
    CAP = 2 * S // E
    G = B * E // P
    BG = B // G
    EQ = P // CAP
    CH = E // EQ
    SLOTS = E * CAP
    ES = B * CAP
    NF = 2 * H
    assert D == P and M == P and T == 2 and H == 2 and S == 256 and HID == P
    assert SLOTS == 512 and ES == 512 and B % 2 == 0 and E % EQ == 0 and G == 2
    N_LD_W = 7 + T
    SCALE = float(DH) ** -0.25
    FEAT_SCALE = float(M) ** -0.5

    with ExitStack() as ctx:
        def sb(name, shape, dt=F32):
            return ctx.enter_context(nc.sbuf_tensor(name, shape, dt))

        def sem(name):
            return ctx.enter_context(nc.semaphore(name))

        bank = [ctx.enter_context(nc.psum_tensor(f"bank{n}", [P, 2, 512], F32)) for n in range(4)]

        def ps(n):
            return bank[n // 2][:, n % 2, :]

        ident = sb("ident", [P, P])
        mask = sb("mask", [P, H, 3 * P])
        minus_half = sb("minus_half", [P, T])
        inner_eps = sb("inner_eps", [P, T])
        ln_eps = sb("ln_eps", [P, T])
        iota_i = sb("iota_i", [P, S], I32)
        iota = sb("iota", [P, S])
        tok_i = sb("tok_i", [P, T], I32)
        tok = sb("tok", [P, T])
        m4 = sb("m4", [P, EQ])
        m16 = sb("m16", [P, E])
        r32 = sb("r32", [P, P // EQ])
        b8 = sb("b8", [P, BG])
        lb = sb("lb", [P, B, P], BF16)
        wqk_raw = sb("wqk_raw", [P, 2, D])
        wqkT = sb("wqkT", [P, 2, D])
        om_raw = sb("om_raw", [P, H, DH])
        omT = sb("omT", [P, M])
        wfeat = sb("wfeat", [P, NF * M])
        wv = sb("wv", [P, D])
        wo = sb("wo", [P, D])
        wf1 = sb("wf1", [P, FF])
        wf2 = sb("wf2", [P, FC, D])
        b1c = sb("b1c", [P, FC])
        b2r = sb("b2r", [P, T, D])
        gam = sb("gam", [P, 1])
        bet = sb("bet", [P, 1])
        rw1 = sb("rw1", [P, HID])
        rw2 = sb("rw2", [P, E])

        span = sb("span", [P, 2 * B * S])
        x_all = span[:, 0:B * S].rearrange("p (b s) -> p b s", b=B)
        x2T_all = span[:, B * S:2 * B * S].rearrange("p (b s) -> p b s", b=B)
        x2_all = sb("x2_all", [P, B, S])
        xs = [sb(f"xs{k}", [P, T, D]) for k in range(2)]
        xT = sb("xT", [P, S])
        vs = [sb(f"vs{k}", [P, T, H, DH + 1]) for k in range(2)]
        negmax = sb("negmax", [P, T * NF])
        z = sb("z", [P, T * NF, M])
        featT = sb("featT", [P, NF, S])
        scores = sb("scores", [P, H, 3 * P])
        den = sb("den", [P, T * H])
        rden = sb("rden", [P, T * H])
        attn = sb("attn", [P, T * H, DH])
        attnT = sb("attnT", [P, S])
        y = sb("y", [P, T, D])
        zhat = sb("zhat", [P, T, D])
        hT = sb("hT", [P, S])
        reluT = sb("reluT", [P, FC, S])
        resid = [sb(f"resid{k}", [P, S]) for k in range(2)]
        y2 = sb("y2", [P, T, D])
        x2s = [sb(f"x2s{k}", [P, T, D]) for k in range(2)]
        stats = [sb(f"stats{k}", [P, T, 6]) for k in range(2)]
        mv = [sb(f"mv{k}", [P, T, 2]) for k in range(2)]
        ve = [sb(f"ve{k}", [P, T]) for k in range(2)]
        rstd = [sb(f"rstd{k}", [P, T]) for k in range(2)]

        silu = [sb(f"silu{k}", [P, 512]) for k in range(2)]
        lgs = [sb(f"lgs{k}", [E, 2 * S]) for k in range(2)]
        lg = sb("lg", [P, G, S])
        nmx = sb("nmx", [P, G])
        ssum = sb("ssum", [P, G])
        rsum = sb("rsum", [P, G])
        val = sb("val", [P, G, CAP])
        idx = sb("idx", [P, G, CAP], U32)
        idxf = sb("idxf", [P, G, CAP])
        wsum = sb("wsum", [P, G])
        wrec = sb("wrec", [P, G])
        wgt = sb("wgt", [P, G, CAP])
        idx4 = sb("idx4", [P, G, EQ, CAP])
        wgt4 = sb("wgt4", [P, G, EQ, CAP])
        r3 = sb("r3", [P, G, E, CAP], BF16)
        slot_tok = sb("slot_tok", [P, B * CH])
        slot_w = sb("slot_w", [P, B * CH])

        hot = [sb(f"hot{k}", [P, T, SLOTS], F32R) for k in range(2)]
        x2h = [sb(f"x2h{k}", [P, T, D], F32R) for k in range(2)]
        x2l = [sb(f"x2l{k}", [P, T, D], F32R) for k in range(2)]
        xg = sb("xg", [P, E, B, CAP])
        wgv = [sb(f"wgv{k}", [P, 2, EF]) for k in range(2)]
        wdn = [sb(f"wdn{k}", [P, EC, D]) for k in range(2)]
        sg = sb("sg", [P, EC, ES])
        hm = [sb(f"hm{k}", [P, EC, ES]) for k in range(2)]
        ys = [sb(f"ys{k}", [P, B // EQ, D]) for k in range(2)]
        y_all = span[:].rearrange("p (c q r d) -> p c q r d", c=CH, q=B // EQ, r=EQ)
        cold = [sb(f"cold{k}", [P, CH, S]) for k in range(2)]
        y3 = [sb(f"y3{k}", [P, T, D]) for k in range(2)]
        outs = [sb(f"outs{k}", [P, T, D]) for k in range(2)]

        s_ld_feat = sem("s_ld_feat")
        s_ld_w = sem("s_ld_w")
        s_ld_r = sem("s_ld_r")
        s_xs = [sem(f"s_xs{k}") for k in range(2)]
        s_x_all = sem("s_x_all")
        s_const = sem("s_const")
        s_sel = sem("s_sel")
        s_prep_pe = sem("s_prep_pe")
        s_prep_ev = sem("s_prep_ev")
        s_xt = sem("s_xt"); s_xT = sem("s_xT")
        s_proj0 = sem("s_proj0"); s_proj1 = sem("s_proj1")
        s_negmax = sem("s_negmax"); s_z = sem("s_z"); s_exp = sem("s_exp")
        s_v = sem("s_v"); s_vs = sem("s_vs")
        s_ft0 = sem("s_ft0"); s_ft1 = sem("s_ft1"); s_feat = sem("s_feat")
        s_sc = sem("s_sc"); s_scores = sem("s_scores")
        s_av = sem("s_av"); s_den = sem("s_den"); s_rden = sem("s_rden"); s_attn = sem("s_attn")
        s_at = sem("s_at"); s_attnT = sem("s_attnT")
        s_wo = sem("s_wo"); s_y = sem("s_y"); s_st = sem("s_st"); s_mv = sem("s_mv")
        s_ve = sem("s_ve"); s_rstd = sem("s_rstd"); s_zhat = sem("s_zhat")
        s_zt = sem("s_zt"); s_hT = sem("s_hT")
        s_f1a = sem("s_f1a"); s_f1b = sem("s_f1b"); s_relu = sem("s_relu")
        s_f2 = sem("s_f2"); s_resid = sem("s_resid"); s_y2 = sem("s_y2")
        s_st2 = sem("s_st2"); s_mv2 = sem("s_mv2"); s_ve2 = sem("s_ve2"); s_rstd2 = sem("s_rstd2")
        s_x2 = sem("s_x2"); s_x2cp = sem("s_x2cp"); s_x2t = sem("s_x2t"); s_x2T = sem("s_x2T")
        s_hid = sem("s_hid"); s_silu = sem("s_silu"); s_lgp = sem("s_lgp"); s_lgs = sem("s_lgs")
        s_lst = [sem(f"s_lst{k}") for k in range(2)]
        s_lg = sem("s_lg")
        s_top = sem("s_top"); s_texp = sem("s_texp"); s_tpe = sem("s_tpe"); s_maps = sem("s_maps")
        s_bc = sem("s_bc"); s_hot = sem("s_hot"); s_x2h = sem("s_x2h"); s_x2l = sem("s_x2l")
        s_g = sem("s_g"); s_xg = sem("s_xg")
        s_ew = [sem(f"s_ew{k}") for k in range(2)]
        s_gv0 = sem("s_gv0"); s_gv1 = sem("s_gv1"); s_sg0 = sem("s_sg0"); s_sg1 = sem("s_sg1")
        s_h0 = sem("s_h0"); s_h1 = sem("s_h1"); s_yp = sem("s_yp"); s_ys = sem("s_ys")
        s_perm = [sem(f"s_perm{k}") for k in range(2)]
        s_cold = sem("s_cold"); s_c = sem("s_c"); s_y3 = sem("s_y3"); s_st3 = sem("s_st3")
        s_mv3 = sem("s_mv3"); s_ve3 = sem("s_ve3"); s_rstd3 = sem("s_rstd3"); s_fin = sem("s_fin")
        s_out = [sem(f"s_out{k}") for k in range(2)]

        def after(eng, s, n):
            if isinstance(n, int) and n < 0:
                return
            eng.wait_ge(s, n + 1)

        def live(n, count):
            return not isinstance(n, int) or 0 <= n < count

        def pipeline(eng, body, count, before, behind):
            lo = 4
            hi = (count - before) // 2 * 2
            for i in range(-before, lo):
                body(i, i // 2, i % 2)
            with eng.Fori(lo // 2, hi // 2) as h:
                for k in range(2):
                    body(h * 2 + k, h, k)
            for i in range(hi, count + behind):
                body(i, i // 2, i % 2)

        block = ctx.enter_context(nc.Block())

        @block.sync
        def _(sp):
            x_t = x.rearrange("b (t p) d -> b p t d", p=P)

            def fixed(n):
                return n if isinstance(n, int) else sp.snap(n)

            for h in range(H):
                sp.dma_start(om_raw[:, h, :], omega).then_inc(s_ld_feat, 16)
            sp.dma_start(wqk_raw[:, 0, :], Wq).then_inc(s_ld_feat, 16)
            sp.dma_start(wqk_raw[:, 1, :], Wk).then_inc(s_ld_feat, 16)
            sp.dma_start(xs[0][:], x_t[0]).then_inc(s_xs[0], 16)
            sp.dma_start(xs[1][:], x_t[1]).then_inc(s_xs[1], 16)
            for t in range(T):
                sp.dma_start(x_all[:, :, t * D:(t + 1) * D],
                             x[:, t * P:(t + 1) * P, :].rearrange("b p d -> p b d")).then_inc(s_x_all, 16)

            with sp.Fori(1, B // 2) as h:
                for k in range(2):
                    i, step = sp.snap(h * 2 + k), sp.snap(h * 2 + (k - 1))
                    sp.wait_ge(s_xt, step)
                    sp.dma_start(xs[k][:], x[ds(i, 1)].rearrange("b (t p) d -> p (b t) d", p=P)).then_inc(s_xs[k], 16)

            def load_expert(e, k):
                e = ds(fixed(e), 1)
                sp.dma_start(wgv[k][:, 0, :], w1[e].rearrange("e d f -> d (e f)")).then_inc(s_ew[k], 16)
                sp.dma_start(wgv[k][:, 1, :], w2[e].rearrange("e d f -> d (e f)")).then_inc(s_ew[k], 16)
                sp.dma_start(wdn[k][:], w3[e].rearrange("e (c p) d -> p (e c) d", p=P)).then_inc(s_ew[k], 16)

            load_expert(0, 0)
            load_expert(1, 1)

            with sp.Fori(0, B // 4) as h:
                for k in range(2):
                    for r in range(2):
                        b = sp.snap(h * 4 + (2 * k + r))
                        if r == 0:
                            done = sp.snap(h * 2 + (k + 1))
                            sp.wait_ge(s_lgs, done)
                        sp.dma_start(logits[ds(b, 1)].rearrange("b e s -> (b e) s"),
                                     lgs[k][:, r * S:(r + 1) * S]).then_inc(s_lst[k], 16)
            for k in range(2):
                sp.wait_ge(s_lst[k], 16 * 2 * (B // 4))
            for g in range(G):
                sp.dma_start(lg[:, g, :], logits[g * BG:(g + 1) * BG].rearrange("b e s -> (b e) s")).then_inc(s_lg, 16)

            def regroup(c, j):
                k = j % 2
                chunk, done = ds(fixed(c + 0), 1), fixed(c * EQ + (j + 1))
                sp.wait_ge(s_ys, done)
                for r in range(EQ):
                    sp.dma_start(y_all[CAP * j:CAP * (j + 1), chunk, :, r, :].rearrange("p c q d -> p (c q) d"),
                                 ys[k][CAP * r:CAP * (r + 1), :, :]).then_inc(s_perm[k], 16)

            with sp.Fori(0, CH - 1) as c:
                for j in range(EQ):
                    regroup(c, j)
                    load_expert(c * EQ + (j + 2), j % 2)
            for j in range(EQ):
                regroup(CH - 1, j)
                if j + 2 < EQ:
                    load_expert((CH - 1) * EQ + j + 2, j % 2)

            with sp.Fori(0, B // 2) as h:
                for k in range(2):
                    b, done = sp.snap(h * 2 + k), sp.snap(h * 2 + (k + 1))
                    sp.wait_ge(s_fin, done)
                    sp.dma_start(out[ds(b, 1)].rearrange("b (t p) d -> p (b t) d", p=P), outs[k][:]).then_inc(s_out[k], 16)
            for k in range(2):
                sp.wait_ge(s_out[k], 16 * (B // 2))

        @block.gpsimd
        def _(pool):
            pool.memset(ident[:], 0.0).then_inc(s_const, 1)
            pool.memset(mask[:], 1.0).then_inc(s_const, 1)
            pool.memset(minus_half[:], -0.5).then_inc(s_const, 1)
            pool.memset(inner_eps[:], INNER_EPS).then_inc(s_const, 1)
            pool.memset(ln_eps[:], LN_EPS).then_inc(s_const, 1)
            for k in range(2):
                pool.memset(vs[k][:, :, :, DH:DH + 1], 1.0).then_inc(s_const, 1)
            pool.iota(iota_i[:], pattern=[[1, S]], base=0, channel_multiplier=0).then_inc(s_const, 1)
            pool.iota(tok_i[:], pattern=[[P, T]], base=0, channel_multiplier=1).then_inc(s_const, 1)
            pool.wait_ge(s_const, 9)
            pool.affine_select(out=ident[:], in_=ident[:], compare_op=ALU.not_equal, fill=1.0,
                               base=0, pattern=[[-1, P]], channel_multiplier=1).then_inc(s_const, 1)
            for h in range(H):
                for n in (0, 2):
                    part = mask[:, h, n * P:(n + 1) * P]
                    pool.affine_select(out=part, in_=part, compare_op=ALU.is_ge, fill=0.0,
                                       base=0, pattern=[[1, P]], channel_multiplier=-1).then_inc(s_const, 1)

            pool.wait_ge(s_ld_w, 16 * N_LD_W)
            pool.wait_ge(s_x_all, 16 * T)

            def inv_std(i, s_var, s_eps, s_done, q, eps):
                after(pool, s_var, i)
                pool.tensor_tensor(ve[q][:], mv[q][:, :, 1], eps[:], ALU.add).then_inc(s_eps, 1)
                after(pool, s_eps, i)
                pool.tensor_tensor(rstd[q][:], ve[q][:], minus_half[:], ALU.pow).then_inc(s_done, 1)

            def layer(i, h, k):
                if live(i - 2, B):
                    after(pool, s_x2, i - 2)
                    n = i - 2
                    pool.tensor_copy(x2_all[:, ds(n, 1), :],
                                     x2s[k][:].rearrange("p t d -> p (t d)").unsqueeze(1)).then_inc(s_x2cp, 1)
                if live(i, B):
                    after(pool, s_y2, i - 2)
                    pool.tensor_tensor(resid[k][:].unsqueeze(1), x_all[:, ds(i, 1), :],
                                       b2r[:].rearrange("p t d -> p (t d)").unsqueeze(1), ALU.add).then_inc(s_resid, 1)
                if live(i - 1, B):
                    after(pool, s_x2, i - 2)
                    inv_std(i - 1, s_mv2, s_ve2, s_rstd2, 1, ln_eps)
                if live(i, B):
                    after(pool, s_zhat, i - 1)
                    inv_std(i, s_mv, s_ve, s_rstd, 0, inner_eps)

            pipeline(pool, layer, B, 2, 2)

            def gather(i, h, k):
                if live(i, B):
                    after(pool, s_x2h, i)
                    after(pool, s_g, i - 2)
                    pool.tensor_tensor(x2l[k][:].rearrange("p t d -> p (t d)").unsqueeze(1), x2_all[:, ds(i, 1), :],
                                       x2h[k][:].bitcast(F32).rearrange("p t d -> p (t d)").unsqueeze(1),
                                       ALU.subtract).then_inc(s_x2l, 1)

            pipeline(pool, gather, B, 0, 0)

            def scatter(i, h, k):
                if live(i, B):
                    after(pool, s_fin, i - 2)
                    inv_std(i, s_mv3, s_ve3, s_rstd3, k, ln_eps)

            pipeline(pool, scatter, B, 0, 0)

        @block.scalar
        def _(act):
            act.dma_start(wv[:], Wv).then_inc(s_ld_w, 16)
            act.dma_start(wo[:], Wo).then_inc(s_ld_w, 16)
            act.dma_start(wf1[:], W1).then_inc(s_ld_w, 16)
            act.dma_start(wf2[:], W2.rearrange("(c p) d -> p c d", p=P)).then_inc(s_ld_w, 16)
            with nc.allow_non_contiguous_dma(reason="bias and scale vectors as columns"):
                act.dma_start(b1c[:], b1.rearrange("(c p) -> p c", p=P)).then_inc(s_ld_w, 16)
                act.dma_start(gam[:], gamma.rearrange("(p a) -> p a", a=1)).then_inc(s_ld_w, 16)
                act.dma_start(bet[:], beta.rearrange("(p a) -> p a", a=1)).then_inc(s_ld_w, 16)
            for t in range(T):
                act.dma_start(b2r[:, t, :], b2.rearrange("(a d) -> a d", a=1).to_broadcast([P, D])).then_inc(s_ld_w, 16)
            act.dma_start(rw1[:], router_w1).then_inc(s_ld_r, 16)
            act.dma_start(rw2[:], router_w2).then_inc(s_ld_r, 16)

            act.wait_ge(s_ld_w, 16 * N_LD_W)

            def layer(i, h, k):
                if live(i, B):
                    after(act, s_ft0, i)
                    act.activation(featT[:, 0:H, :].rearrange("p f s -> p (f s)"), ps(2), ACT.Copy, bias=FEAT_EPS, scale=FEAT_SCALE)
                    after(act, s_ft1, i)
                    act.activation(featT[:, H:, :].rearrange("p f s -> p (f s)"), ps(3), ACT.Copy, bias=FEAT_EPS,
                                   scale=FEAT_SCALE).then_inc(s_feat, 1)
                if live(i + 1, B):
                    after(act, s_v, i + 1)
                    act.activation(vs[1 - k][:, :, :, 0:DH], ps(6)[:, 0:T * D].rearrange("p (t h d) -> p t h d", t=T, h=H),
                                   ACT.Copy).then_inc(s_vs, 1)
                if live(i - 1, B):
                    for c in range(FC):
                        if c % 2 == 0:
                            after(act, (s_f1a, s_f1b)[c // 2], i - 1)
                        op = act.activation(reluT[:, c, :], ps(2 + c // 2)[:, c % 2 * S:(c % 2 + 1) * S], ACT.Relu,
                                            bias=b1c[:, c:c + 1])
                    op.then_inc(s_relu, 1)
                if live(i + 1, B):
                    after(act, s_z, i + 1)
                    act.activation(z[:], z[:], ACT.Exp).then_inc(s_exp, 1)
                if live(i, B):
                    after(act, s_at, i)
                    act.activation(attnT[:], ps(5)[:, 0:S], ACT.Copy).then_inc(s_attnT, 1)
                if live(i - 2, B):
                    after(act, s_x2t, i - 2)
                    act.activation(x2T_all[:, ds(i - 2, 1), :], ps(5)[:, 0:S].unsqueeze(1), ACT.Copy).then_inc(s_x2T, 1)
                if live(i + 2, B):
                    after(act, s_xt, i + 2)
                    act.activation(xT[:], ps(0)[:, 0:S], ACT.Copy).then_inc(s_xT, 1)

            pipeline(act, layer, B, 2, 2)

            def router(q, h, k):
                if live(q, B // 2):
                    after(act, s_hid, q)
                    act.activation(silu[k][:], ps(k), ACT.Silu).then_inc(s_silu, 1)

            pipeline(act, router, B // 2, 0, 0)

            act.wait_ge(s_top, 1)
            for g in range(G):
                act.activation(lg[:, g, :], lg[:, g, :], ACT.Exp, bias=nmx[:, g:g + 1],
                               accum_out=ssum[:, g:g + 1]).then_inc(s_texp, 1)

            def gather(i, h, k):
                if live(i, B):
                    after(act, s_g, i - 2)
                    act.activation(x2h[k][:].rearrange("p t d -> p (t d)").unsqueeze(1), x2_all[:, ds(i, 1), :],
                                   ACT.Copy).then_inc(s_x2h, 1)
                if live(i - 1, B):
                    after(act, s_g, i - 1)
                    act.activation(xg[:, :, ds(i - 1, 1), :].rearrange("p e b c -> p (e b) c"),
                                   ps(3 - k).rearrange("p (e c) -> p e c", e=E), ACT.Copy).then_inc(s_xg, 1)

            act.wait_ge(s_x2cp, B)
            pipeline(act, gather, B, 0, 1)

            def expert(e, h, k):
                if live(e, E):
                    after(act, s_gv0, e)
                    after(act, s_h0, e - 1)
                    act.activation(sg[:, 0, :], ps(0), ACT.Silu).then_inc(s_sg0, 1)
                if live(e - 1, E):
                    after(act, s_yp, e - 1)
                    regrouped(act, e - 1, h - 1 if k == 0 else h, 1 - k)
                    act.activation(ys[1 - k][:].rearrange("p q d -> p (q d)"), ps(5 - k), ACT.Copy).then_inc(s_ys, 1)
                if live(e, E):
                    after(act, s_gv1, e)
                    after(act, s_h1, e - 1)
                    act.activation(sg[:, 1, :], ps(2), ACT.Silu).then_inc(s_sg1, 1)

            def regrouped(eng, e, turn, k):
                if isinstance(e, int) and e < 2:
                    return
                eng.wait_ge(s_perm[k], turn * (16 * EQ))

            pipeline(act, expert, E, 0, 1)

        @block.vector
        def _(dve):
            dve.wait_ge(s_const, 10 + 2 * H)
            dve.tensor_reduce(m4[:], ident[:].rearrange("p (q j) -> p j q", j=EQ), AX.X, ALU.add).then_inc(s_sel, 1)
            dve.tensor_reduce(r32[:], ident[:].rearrange("p (q j) -> p q j", j=EQ), AX.X, ALU.add).then_inc(s_sel, 1)
            dve.tensor_reduce(m16[:], ident[:].rearrange("p (b e) -> p e b", e=E), AX.X, ALU.add).then_inc(s_sel, 1)
            dve.tensor_reduce(b8[:], ident[:].rearrange("p (b e) -> p b e", e=E), AX.X, ALU.add).then_inc(s_sel, 1)
            dve.tensor_copy(iota[:], iota_i[:]).then_inc(s_sel, 1)
            dve.tensor_copy(tok[:], tok_i[:]).then_inc(s_sel, 1)
            dve.wait_ge(s_sel, 4)
            for g in range(G):
                dve.tensor_copy(lb[:, g * BG:(g + 1) * BG, :], b8[:].unsqueeze(2).to_broadcast([P, BG, P])).then_inc(s_sel, 1)

            dve.wait_ge(s_prep_pe, 1)
            dve.tensor_copy(wqkT[:].rearrange("p n d -> p (n d)"), ps(0)[:, 0:2 * D]).then_inc(s_prep_ev, 1)
            dve.tensor_copy(omT[:], ps(0)[:, 2 * D:2 * D + M]).then_inc(s_prep_ev, 1)
            dve.wait_ge(s_prep_pe, 2)
            for h in range(H):
                dve.tensor_scalar(wfeat[:].rearrange("p (n h m) -> p n h m", n=2, h=H)[:, :, h, :],
                                  ps(1 + h)[:, 0:2 * M].rearrange("p (n m) -> p n m", n=2), SCALE, None,
                                  ALU.mult).then_inc(s_prep_ev, 1)

            dve.wait_ge(s_ld_w, 16 * N_LD_W)
            dve.wait_ge(s_x_all, 16 * T)

            def sums(src, q, s_stats):
                for t in range(T):
                    op = dve.bn_stats(stats[q][:, t, :], src[:, t, :])
                op.then_inc(s_stats, 1)

            def moments(q, s_done):
                for t in range(T):
                    op = dve.bn_aggr(mv[q][:, t, :], stats[q][:, t, :])
                op.then_inc(s_done, 1)

            def normalise(dst, src, q, s_done):
                for t in range(T):
                    op = dve.tensor_scalar(dst[:, t, :], src[:, t, :], mv[q][:, t, 0:1], rstd[q][:, t:t + 1],
                                           ALU.subtract, ALU.mult)
                op.then_inc(s_done, 1)

            def layer(i, h, k):
                if live(i + 1, B):
                    after(dve, s_proj0, i + 1)
                    dve.tensor_reduce(negmax[:, 0:NF], ps(0).rearrange("p (f m) -> p f m", f=NF), AX.X, ALU.max,
                                      negate=True)
                    after(dve, s_proj1, i + 1)
                    dve.tensor_reduce(negmax[:, NF:], ps(1).rearrange("p (f m) -> p f m", f=NF), AX.X, ALU.max,
                                      negate=True).then_inc(s_negmax, 1)
                if live(i - 1, B):
                    after(dve, s_zt, i - 1)
                    dve.tensor_scalar(hT[:], ps(7)[:, 0:S], gam[:], bet[:], ALU.mult, ALU.add).then_inc(s_hT, 1)
                if live(i, B):
                    after(dve, s_sc, i)
                    dve.tensor_tensor(scores[:], bank[2][:, :, 0:3 * P], mask[:], ALU.mult).then_inc(s_scores, 1)
                if live(i + 1, B):
                    after(dve, s_negmax, i + 1)
                    dve.tensor_tensor(z[:], bank[0][:].rearrange("p t (f m) -> p (t f) m", f=NF),
                                      negmax[:].unsqueeze(2).to_broadcast([P, T * NF, M]), ALU.add).then_inc(s_z, 1)
                if live(i, B):
                    after(dve, s_av, i)
                    av = ps(4)[:, 0:T * H * (DH + 1)].rearrange("p (g d) -> p g d", d=DH + 1)
                    dve.tensor_scalar(den[:].unsqueeze(2), av[:, :, DH:DH + 1], FEAT_EPS, None, ALU.add).then_inc(s_den, 1)
                    after(dve, s_den, i)
                    dve.reciprocal(rden[:], den[:]).then_inc(s_rden, 1)
                    after(dve, s_rden, i)
                    dve.tensor_tensor(attn[:], av[:, :, 0:DH], rden[:].unsqueeze(2).to_broadcast([P, T * H, DH]),
                                      ALU.mult).then_inc(s_attn, 1)
                if live(i - 1, B):
                    after(dve, s_f2, i - 1)
                    after(dve, s_resid, i - 1)
                    dve.tensor_tensor(y2[:].rearrange("p t d -> p (t d)"), ps(7)[:, 0:S], resid[1 - k][:],
                                      ALU.add).then_inc(s_y2, 1)
                    after(dve, s_y2, i - 1)
                    sums(y2, 1, s_st2)
                    after(dve, s_st2, i - 1)
                if live(i, B):
                    after(dve, s_wo, i)
                    dve.tensor_tensor(y[:].rearrange("p t d -> p (t d)").unsqueeze(1), ps(6)[:, 0:S].unsqueeze(1),
                                      x_all[:, ds(i, 1), :], ALU.add).then_inc(s_y, 1)
                if live(i - 1, B):
                    moments(1, s_mv2)
                if live(i, B):
                    after(dve, s_y, i)
                    sums(y, 0, s_st)
                    after(dve, s_st, i)
                if live(i - 1, B):
                    after(dve, s_rstd2, i - 1)
                    after(dve, s_x2t, i - 3)
                    after(dve, s_x2cp, i - 3)
                    normalise(x2s[1 - k], y2, 1, s_x2)
                if live(i, B):
                    moments(0, s_mv)
                    after(dve, s_rstd, i)
                    normalise(zhat, y, 0, s_zhat)

            pipeline(dve, layer, B, 2, 2)

            def router(q, h, k):
                if live(q - 1, B // 2):
                    after(dve, s_lgp, q - 1)
                    stored(dve, q - 1, h if k else h - 1, 1 - k)
                    dve.tensor_copy(lgs[1 - k][:], ps(3 - k)[0:E, :]).then_inc(s_lgs, 1)

            def stored(eng, q, turn, k):
                if isinstance(q, int) and q < 2:
                    return
                eng.wait_ge(s_lst[k], turn * 32)

            pipeline(dve, router, B // 2, 0, 1)

            dve.wait_ge(s_lg, 16 * G)
            dve.tensor_reduce(nmx[:], lg[:], AX.X, ALU.max, negate=True).then_inc(s_top, 1)
            dve.wait_ge(s_texp, G)
            done = 1

            def step(ins):
                nonlocal done
                done += 1
                ins.then_inc(s_top, 1)
                dve.wait_ge(s_top, done)

            step(dve.reciprocal(rsum[:], ssum[:]))
            step(dve.tensor_tensor(lg[:], lg[:], rsum[:].unsqueeze(2).to_broadcast([P, G, S]), ALU.mult))
            for r in range(CAP // 8):
                for g in range(G):
                    top = val[:, g, 8 * r:8 * r + 8]
                    step(dve.max(top, lg[:, g, :]))
                    step(dve.max_index(idx[:, g, 8 * r:8 * r + 8], top, lg[:, g, :]))
                    if r < CAP // 8 - 1:
                        step(dve.match_replace(lg[:, g, :], top, lg[:, g, :], -1.0))
            step(dve.tensor_reduce(wsum[:], val[:], AX.X, ALU.add))
            step(dve.tensor_scalar(wsum[:], wsum[:], WEIGHT_EPS, None, ALU.add))
            step(dve.reciprocal(wrec[:], wsum[:]))
            step(dve.tensor_tensor(wgt[:], val[:], wrec[:].unsqueeze(2).to_broadcast([P, G, CAP]), ALU.mult))
            step(dve.tensor_copy(idxf[:], idx[:]))
            for g in range(G):
                dve.tensor_tensor(r3[:, g], idxf[:, g].unsqueeze(1).to_broadcast([P, E, CAP]),
                                  m16[:].unsqueeze(2).to_broadcast([P, E, CAP]), ALU.mult)
                dve.tensor_tensor(idx4[:, g], idxf[:, g].unsqueeze(1).to_broadcast([P, EQ, CAP]),
                                  m4[:].unsqueeze(2).to_broadcast([P, EQ, CAP]), ALU.mult)
                op = dve.tensor_tensor(wgt4[:, g], wgt[:, g].unsqueeze(1).to_broadcast([P, EQ, CAP]),
                                       m4[:].unsqueeze(2).to_broadcast([P, EQ, CAP]), ALU.mult)
            op.then_inc(s_tpe, 1)
            dve.wait_ge(s_tpe, 2)
            half = B * CH
            dve.tensor_copy(slot_tok[:], ps(0)[:, 0:half]).then_inc(s_maps, 1)
            dve.tensor_copy(slot_w[:], ps(1)[:, 0:half]).then_inc(s_maps, 1)

            def gather(i, h, k):
                if live(i, B):
                    after(dve, s_bc, i)
                    after(dve, s_g, i - 2)
                    for t in range(T):
                        op = dve.tensor_scalar(hot[k][:, t, :], ps(k), tok[:, t:t + 1], None, ALU.is_equal)
                    op.then_inc(s_hot, 1)

            pipeline(dve, gather, B, 0, 0)

            def expert(e, h, k):
                if live(e, E):
                    after(dve, s_yp, e - 2)
                    after(dve, s_sg0, e)
                    dve.tensor_tensor(hm[k][:, 0, :], sg[:, 0, :], ps(1), ALU.mult).then_inc(s_h0, 1)
                    after(dve, s_sg1, e)
                    dve.tensor_tensor(hm[k][:, 1, :], sg[:, 1, :], ps(3), ALU.mult).then_inc(s_h1, 1)

            pipeline(dve, expert, E, 0, 0)

            def cold_maps(i, k):
                after(dve, s_c, i - 2)
                for c in range(CH):
                    col = ds(i * CH + c, 1)
                    op = dve.tensor_scalar(cold[k][:, c, :], iota[:], slot_tok[:, col], slot_w[:, col],
                                           ALU.is_equal, ALU.mult)
                op.then_inc(s_cold, 1)

            def scatter(i, h, k):
                if live(i + 1, B):
                    cold_maps(i + 1, 1 - k)
                if live(i, B):
                    after(dve, s_c, i)
                    after(dve, s_fin, i - 2)
                    dve.tensor_tensor(y3[k][:].rearrange("p t d -> p (t d)").unsqueeze(1), ps(k)[:, 0:S].unsqueeze(1),
                                      x2_all[:, ds(i, 1), :], ALU.add).then_inc(s_y3, 1)
                    after(dve, s_y3, i)
                    sums(y3[k], k, s_st3)
                    after(dve, s_st3, i)
                if live(i - 1, B):
                    after(dve, s_rstd3, i - 1)
                    if not isinstance(i, int) or i >= 3:
                        dve.wait_ge(s_out[1 - k], (h * 16 if k else h * 16 - 16))
                    normalise(outs[1 - k], y3[1 - k], 1 - k, s_fin)
                if live(i, B):
                    moments(k, s_mv3)

            pipeline(dve, scatter, B, 1, 1)

        @block.tensor
        def _(pe):
            pe.wait_ge(s_const, 10 + 2 * H)
            pe.wait_ge(s_ld_feat, 16 * (2 + H))
            for n in range(2):
                pe.transpose(ps(0)[:, n * D:(n + 1) * D], wqk_raw[:, n, :], ident[:])
            pe.transpose(ps(0)[:, 2 * D:2 * D + M], om_raw[:].rearrange("p h d -> p (h d)"), ident[:]).then_inc(s_prep_pe, 1)
            pe.wait_ge(s_prep_ev, 2)
            for n in range(2):
                for h in range(H):
                    op = pe.matmul(ps(1 + h)[:, n * M:(n + 1) * M], wqkT[h * DH:(h + 1) * DH, n, :],
                                   omT[h * DH:(h + 1) * DH, :], start=True, stop=True)
            op.then_inc(s_prep_pe, 1)

            def transposes(dst, src, s):
                for t in range(T):
                    op = pe.transpose(dst[:, t * P:(t + 1) * P], src[:, t, :], ident[:])
                op.then_inc(s, 1)

            def features(i):
                after(pe, s_exp, i)
                for f in range(NF):
                    for t in range(T):
                        op = pe.transpose(ps(2 + f // 2)[:, f % 2 * S + t * P:f % 2 * S + (t + 1) * P],
                                          z[:, t * NF + f, :], ident[:])
                    if f % 2:
                        op.then_inc((s_ft0, s_ft1)[f // 2], 1)

            def project(i):
                after(pe, s_xT, i)
                for t in range(T):
                    pe.matmul(ps(t), xT[:, t * P:(t + 1) * P], wfeat[:], start=True, stop=True)\
                      .then_inc((s_proj0, s_proj1)[t], 1)
                after(pe, s_y, i - 2)
                for t in range(T):
                    op = pe.matmul(ps(6)[:, t * D:(t + 1) * D], xT[:, t * P:(t + 1) * P], wv[:], start=True, stop=True)
                op.then_inc(s_v, 1)

            def qk(i):
                after(pe, s_feat, i)
                after(pe, s_x2T, i - 3)
                for h in range(H):
                    q, kf, to = featT[:, h, :], featT[:, H + h, :], ps(4 + h)
                    pe.matmul(to[:, 0:S], kf[:, 0:P], q, start=True, stop=True)
                    op = pe.matmul(to[:, S:S + P], kf[:, P:S], q[:, P:S], start=True, stop=True)
                op.then_inc(s_sc, 1)

            def attend(i, k):
                after(pe, s_scores, i)
                after(pe, s_vs, i)
                w = DH + 1
                for h in range(H):
                    pe.matmul(ps(4)[:, h * w:(h + 1) * w], scores[:, h, 0:P], vs[k][:, 0, h, :], start=True, stop=True)
                    to = ps(4)[:, (H + h) * w:(H + h + 1) * w]
                    pe.matmul(to, scores[:, h, P:2 * P], vs[k][:, 0, h, :], start=True, stop=False)
                    op = pe.matmul(to, scores[:, h, 2 * P:3 * P], vs[k][:, 1, h, :], start=False, stop=True)
                op.then_inc(s_av, 1)

            def ffn_up(i):
                after(pe, s_hT, i)
                for c in range(FC):
                    op = pe.matmul(ps(2 + c // 2)[:, c % 2 * S:(c % 2 + 1) * S], wf1[:, c * P:(c + 1) * P], hT[:],
                                   start=True, stop=True)
                    if c % 2:
                        op.then_inc((s_f1a, s_f1b)[c // 2], 1)

            def ffn_down(i, t):
                for c in range(FC):
                    op = pe.matmul(ps(7)[:, t * D:(t + 1) * D], reluT[:, c, t * P:(t + 1) * P], wf2[:, c, :],
                                   start=(c == 0), stop=(c == FC - 1))
                if t == T - 1:
                    op.then_inc(s_f2, 1)

            def layer(i, h, k):
                if live(i, B):
                    features(i)
                if live(i + 1, B):
                    project(i + 1)
                if live(i - 1, B):
                    after(pe, s_zhat, i - 1)
                    after(pe, s_y2, i - 2)
                    transposes(ps(7), zhat, s_zt)
                if live(i, B):
                    qk(i)
                if live(i - 1, B):
                    ffn_up(i - 1)
                if live(i, B):
                    attend(i, k)
                if live(i - 1, B):
                    after(pe, s_relu, i - 1)
                    ffn_down(i - 1, 0)
                if live(i, B):
                    after(pe, s_attn, i)
                    transposes(ps(5), attn[:].rearrange("p (t h) d -> p t (h d)", t=T), s_at)
                if live(i - 1, B):
                    ffn_down(i - 1, 1)
                if live(i, B):
                    after(pe, s_attnT, i)
                    if live(i + 1, B):
                        after(pe, s_vs, i + 1)
                    for t in range(T):
                        op = pe.matmul(ps(6)[:, t * D:(t + 1) * D], attnT[:, t * P:(t + 1) * P], wo[:],
                                       start=True, stop=True)
                    op.then_inc(s_wo, 1)
                if live(i - 2, B):
                    after(pe, s_x2, i - 2)
                    if not live(i, B):
                        after(pe, s_x2T, i - 3)
                    transposes(ps(5), x2s[k], s_x2t)
                if live(i + 2, B):
                    if isinstance(i, int):
                        pe.wait_ge(s_xs[k], 16 * (h + 2))
                    else:
                        pe.wait_ge(s_xs[k], h * 16 + 32)
                    if live(i + 1, B):
                        after(pe, s_z, i + 1)
                    transposes(ps(0), xs[k], s_xt)

            pe.wait_ge(s_prep_ev, 2 + H)
            pe.wait_ge(s_ld_w, 16 * N_LD_W)
            pipeline(pe, layer, B, 2, 2)

            def router(q, h, k):
                if live(q + 1, B // 2):
                    after(pe, s_silu, q - 1)
                    n = q + 1
                    src = x2T_all[:, ds(2 * n if isinstance(n, int) else n * 2, 2), :]
                    pe.matmul(ps(1 - k), rw1[:], src, start=True, stop=True).then_inc(s_hid, 1)
                if live(q, B // 2):
                    after(pe, s_silu, q)
                    after(pe, s_lgs, q - 2)
                    pe.matmul(ps(2 + k)[0:E, :], rw2[:], silu[k][:], start=True, stop=True).then_inc(s_lgp, 1)

            pe.wait_ge(s_ld_r, 32)
            pe.wait_ge(s_x2T, B)
            pipeline(pe, router, B // 2, 1, 0)

            pe.wait_ge(s_tpe, 1)
            for g in range(G):
                cols = slice(g * P // EQ, (g + 1) * P // EQ)
                pe.matmul(ps(0)[:, cols], idx4[:, g].rearrange("p j c -> p (j c)"), r32[:], start=True, stop=True)
                op = pe.matmul(ps(1)[:, cols], wgt4[:, g].rearrange("p j c -> p (j c)"), r32[:], start=True, stop=True)
            op.then_inc(s_tpe, 1)
            pe.wait_ge(s_maps, 2)

            def gather(i, h, k):
                if live(i + 1, B):
                    n = i + 1
                    after(pe, s_hot, i - 1)
                    g = n // BG
                    pe.matmul(ps(1 - k), lb[:, ds(n, 1), :].rearrange("p a m -> p (a m)"),
                              r3[:, ds(g, 1)].rearrange("p a e c -> p (a e c)"), start=True, stop=True).then_inc(s_bc, 1)
                if live(i, B):
                    after(pe, s_hot, i)
                    after(pe, s_x2l, i)
                    after(pe, s_xg, i - 2)
                    for t in range(T):
                        for part in (x2l, x2h):
                            op = pe.matmul(ps(2 + k), part[k][:, t, :], hot[k][:, t, :],
                                           start=(t == 0 and part is x2l), stop=(t == T - 1 and part is x2h))
                    op.then_inc(s_g, 1)

            pipeline(pe, gather, B, 1, 0)

            def expert(e, h, k):
                def gate_value(c, s):
                    src = xg[:, ds(e, 1)].rearrange("p a b c -> p (a b c)")
                    for n in range(2):
                        op = pe.matmul(ps(2 * c + n), wgv[k][:, n, c * P:(c + 1) * P], src, start=True, stop=True)
                    op.then_inc(s, 1)

                if live(e, E):
                    pe.wait_ge(s_ew[k], 48 * (h + 1) if isinstance(e, int) else h * 48 + 48)
                    after(pe, s_h0, e - 1)
                    gate_value(0, s_gv0)
                if live(e - 1, E):
                    after(pe, s_h1, e - 1)
                    after(pe, s_ys, e - 3)
                    for q in range(B // EQ):
                        for c in range(EC):
                            op = pe.matmul(ps(5 - k)[:, q * D:(q + 1) * D], hm[1 - k][:, c, q * P:(q + 1) * P],
                                           wdn[1 - k][:, c, :], start=(c == 0), stop=(c == EC - 1))
                    op.then_inc(s_yp, 1)
                if live(e, E):
                    after(pe, s_h1, e - 1)
                    gate_value(1, s_gv1)

            pe.wait_ge(s_xg, B)
            pipeline(pe, expert, E, 0, 1)

            def scatter(i, h, k):
                if live(i, B):
                    after(pe, s_cold, i)
                    after(pe, s_y3, i - 2)
                    for t in range(T):
                        for c in range(CH):
                            src = y_flat[:, c, ds(i, 1), :].rearrange("p a d -> p (a d)")
                            op = pe.matmul(ps(k)[:, t * D:(t + 1) * D], cold[k][:, c, t * P:(t + 1) * P], src,
                                           start=(c == 0), stop=(c == CH - 1))
                    op.then_inc(s_c, 1)

            y_flat = y_all.rearrange("p c q r d -> p c (q r) d")
            for k in range(2):
                pe.wait_ge(s_perm[k], 16 * EQ * (E // 2))
            pipeline(pe, scatter, B, 0, 0)


_INS = ['L0_attn_batch', 'L0_attn_Wq', 'L0_attn_Wk', 'L0_attn_Wv', 'L0_attn_Wo', 'L0_attn_omega', 'L0_attn_W1',
        'L0_attn_b1', 'L0_attn_W2', 'L0_attn_b2', 'L0_attn_gamma', 'L0_attn_beta', 'L0_ffn_router_w1',
        'L0_ffn_router_w2', 'L0_ffn_w1', 'L0_ffn_w2', 'L0_ffn_w3']


def kernel(**inputs):
    import numpy as _np
    import concourse.bacc as _bacc
    from concourse import mybir as _mybir
    from concourse.bass_utils import run_bass_kernel_spmd as _run

    nc = _bacc.Bacc("TRN2", target_bir_lowering=False, num_devices=1)
    arrays, args = {}, []
    for name in _INS:
        a = _np.ascontiguousarray(inputs[name])
        arrays[f"in_{name}_dram"] = a
        args.append(nc.dram_tensor(f"in_{name}_dram", a.shape, _mybir.dt.from_np(a.dtype), kind="ExternalInput").ap())
    shape = inputs['L0_attn_batch'].shape
    experts = inputs['L0_ffn_w1'].shape[0]
    logits = nc.dram_tensor("router_logits", (shape[0], experts, shape[1]), _mybir.dt.float32, kind="Internal").ap()
    res = nc.dram_tensor("out_0_dram", shape, _mybir.dt.float32, kind="ExternalOutput").ap()
    post_ln_block(nc, *args, logits, res)
    r = _run(nc, [arrays], core_ids=[0])
    return r.results[0]["out_0_dram"]
```

```python
from contextlib import ExitStack

import concourse.bass as bass
from concourse import mybir

ALU = mybir.AluOpType
ACT = mybir.ActivationFunctionType
AX = mybir.AxisListType
F32 = mybir.dt.float32
F32R = mybir.dt.float32r
BF16 = mybir.dt.bfloat16
I32 = mybir.dt.int32
U32 = mybir.dt.uint32
ds = bass.ds

P = 128
INNER_EPS = 1e6
FEAT_EPS = 1e-6
LN_EPS = 1e-5
WEIGHT_EPS = 1e-9


def post_ln_block(nc, x, Wq, Wk, Wv, Wo, omega, W1, b1, W2, b2, gamma, beta,
                  router_w1, router_w2, w1, w2, w3, logits, out):
    B, S, D = x.shape
    M, DH = omega.shape
    H = D // DH
    FF = W1.shape[1]
    FC = FF // P
    E, _, EF = w1.shape
    EC = EF // P
    HID = router_w1.shape[1]
    T = S // P
    CAP = 2 * S // E
    G = B * E // P
    BG = B // G
    EQ = P // CAP
    CH = E // EQ
    SLOTS = E * CAP
    ES = B * CAP
    NF = 2 * H
    assert D == P and M == P and T == 2 and H == 2 and S == 256 and HID == P
    assert SLOTS == 512 and ES == 512 and B % 2 == 0 and E % EQ == 0 and G == 2
    N_LD_W = 7 + T
    SCALE = float(DH) ** -0.25
    FEAT_SCALE = float(M) ** -0.5

    with ExitStack() as ctx:
        early = ctx.enter_context(ExitStack())

        def sb(name, shape, dt=F32, stack=ctx):
            return stack.enter_context(nc.sbuf_tensor(name, shape, dt))

        def eb(name, shape, dt=F32):
            return sb(name, shape, dt, early)

        def sem(name):
            return ctx.enter_context(nc.semaphore(name))

        bank = [ctx.enter_context(nc.psum_tensor(f"bank{n}", [P, 2, 512], F32)) for n in range(4)]

        def ps(n):
            return bank[n // 2][:, n % 2, :]

        ident = sb("ident", [P, P])
        minus_half = sb("minus_half", [P, T])
        inner_eps = sb("inner_eps", [P, T])
        ln_eps = sb("ln_eps", [P, T])
        iota_i = sb("iota_i", [P, S], I32)
        iota = sb("iota", [P, S])
        tok_i = sb("tok_i", [P, T], I32)
        tok = sb("tok", [P, T])
        m4 = sb("m4", [P, EQ])
        m16 = sb("m16", [P, E])
        r32 = sb("r32", [P, P // EQ])
        b8 = sb("b8", [P, BG])
        lb = sb("lb", [P, B, P], BF16)

        x2_all = sb("x2_all", [P, B, S])
        mv = [sb(f"mv{k}", [P, T, 2]) for k in range(3)]
        ve = [sb(f"ve{k}", [P, T]) for k in range(3)]
        rstd = [sb(f"rstd{k}", [P, T]) for k in range(3)]
        stats = [sb(f"stats{k}", [P, T, 6]) for k in range(2)]

        lg = sb("lg", [P, G, S])
        nmx = sb("nmx", [P, G])
        ssum = sb("ssum", [P, G])
        rsum = sb("rsum", [P, G])
        val = sb("val", [P, G, CAP])
        idx = sb("idx", [P, G, CAP], U32)
        idxf = sb("idxf", [P, G, CAP])
        wsum = sb("wsum", [P, G])
        wrec = sb("wrec", [P, G])
        wgt = sb("wgt", [P, G, CAP])
        idx4 = sb("idx4", [P, G, EQ, CAP])
        wgt4 = sb("wgt4", [P, G, EQ, CAP])
        r3 = sb("r3", [P, G, E, CAP], BF16)
        slot_tok = sb("slot_tok", [P, B * CH])
        slot_w = sb("slot_w", [P, B * CH])
        minus_tok = sb("minus_tok", [P, B * CH])
        minus_w = sb("minus_w", [P, B * CH])

        mask = eb("mask", [P, T * H, P])
        wqk_raw = eb("wqk_raw", [P, 2, D])
        wqkT = eb("wqkT", [P, 2, D])
        om_raw = eb("om_raw", [P, H, DH])
        omT = eb("omT", [P, M])
        wfeat = eb("wfeat", [P, NF * M])
        wv = eb("wv", [P, D])
        wo = eb("wo", [P, D])
        wf1 = eb("wf1", [P, FF])
        wf2 = eb("wf2", [P, FC, D])
        b1c = eb("b1c", [P, FC])
        b2r = eb("b2r", [P, T, D])
        gam = eb("gam", [P, 1])
        bet = eb("bet", [P, 1])
        x_all = eb("x_all", [P, B, S])
        xs = [eb(f"xs{k}", [P, T, D]) for k in range(2)]
        xT = eb("xT", [P, S])
        vs = [eb(f"vs{k}", [P, T, H, DH + 1]) for k in range(2)]
        negmax = eb("negmax", [P, T * NF])
        feat = eb("feat", [P, T * NF, M])
        featT = eb("featT", [P, NF, S])
        diag = eb("diag", [P, H * T, P])
        cross = eb("cross", [P, H, P])
        den = eb("den", [P, T * H])
        rden = eb("rden", [P, T * H])
        attn = eb("attn", [P, T * H, DH])
        attnT = eb("attnT", [P, S])
        y = eb("y", [P, T, D])
        zhat = eb("zhat", [P, T, D])
        hT = eb("hT", [P, S])
        reluT = eb("reluT", [P, FC, S])
        resid = [eb(f"resid{k}", [P, S]) for k in range(2)]
        y2 = [eb(f"y2{k}", [P, T, D]) for k in range(2)]
        x2s = [eb(f"x2s{k}", [P, T, D]) for k in range(2)]

        rw1 = eb("rw1", [P, HID])
        rw2 = eb("rw2", [P, E])
        x2T_all = eb("x2T_all", [P, B, S])
        silu = [eb(f"silu{k}", [P, 512]) for k in range(2)]
        lgs = [eb(f"lgs{k}", [E, 2 * S]) for k in range(2)]
        early.close()

        wgv = [sb(f"wgv{j}", [P, 2, EF]) for j in range(EQ)]
        wdn = [sb(f"wdn{j}", [P, EC, D]) for j in range(EQ)]
        wh = [sb(f"wh{k}", [P, 2, EF], F32R) for k in range(2)]
        wl = [sb(f"wl{k}", [P, 2, EF], F32R) for k in range(2)]
        tokens = [sb(f"tokens{k}", [P, SLOTS], BF16) for k in range(2)]
        hot = [sb(f"hot{k}", [P, T, SLOTS], F32R) for k in range(2)]
        x2h = [sb(f"x2h{k}", [P, T, D], F32R) for k in range(2)]
        x2l = [sb(f"x2l{k}", [P, T, D], F32R) for k in range(2)]
        xgh = sb("xgh", [P, E, B, CAP], F32R)
        xgl = sb("xgl", [P, E, B, CAP], F32R)
        sg = sb("sg", [P, EC, ES])
        hm = [sb(f"hm{k}", [P, EC, ES]) for k in range(2)]
        ys = [sb(f"ys{k}", [P, B // EQ, D]) for k in range(2)]
        y_all = sb("y_all", [P, CH, B // EQ, EQ, D])
        cold = [sb(f"cold{k}", [P, CH, S]) for k in range(2)]
        away = [sb(f"away{k}", [P, CH // 2, S]) for k in range(2)]
        y3 = [sb(f"y3{k}", [P, T, D]) for k in range(2)]
        outs = [sb(f"outs{k}", [P, T, D]) for k in range(2)]

        s_ld_feat = sem("s_ld_feat")
        s_ld_w = sem("s_ld_w")
        s_ld_r = sem("s_ld_r")
        s_xs = [sem(f"s_xs{k}") for k in range(2)]
        s_x_all = sem("s_x_all")
        s_const = sem("s_const")
        s_sel = sem("s_sel")
        s_prep_pe = sem("s_prep_pe")
        s_prep_ev = sem("s_prep_ev")
        s_xt = sem("s_xt"); s_xT = sem("s_xT")
        s_proj0 = sem("s_proj0"); s_proj1 = sem("s_proj1")
        s_negmax = sem("s_negmax"); s_exp = sem("s_exp")
        s_v = sem("s_v"); s_vs = sem("s_vs")
        s_ft0 = sem("s_ft0"); s_ft1 = sem("s_ft1"); s_feat = sem("s_feat")
        s_sc = sem("s_sc"); s_diag = sem("s_diag"); s_cross = sem("s_cross")
        s_av = sem("s_av"); s_den = sem("s_den"); s_rden = sem("s_rden"); s_attn = sem("s_attn")
        s_at = sem("s_at"); s_attnT = sem("s_attnT")
        s_wo = sem("s_wo"); s_y = sem("s_y"); s_st = sem("s_st"); s_mv = sem("s_mv")
        s_ve = sem("s_ve"); s_rstd = sem("s_rstd"); s_zhat = sem("s_zhat")
        s_zt = sem("s_zt"); s_hT = sem("s_hT")
        s_f1a = sem("s_f1a"); s_f1b = sem("s_f1b"); s_relu = sem("s_relu")
        s_f2 = sem("s_f2"); s_resid = sem("s_resid"); s_y2 = sem("s_y2")
        s_st2 = sem("s_st2"); s_mv2 = sem("s_mv2"); s_ve2 = sem("s_ve2"); s_rstd2 = sem("s_rstd2")
        s_x2 = sem("s_x2"); s_x2cp = sem("s_x2cp"); s_x2t = sem("s_x2t"); s_x2T = sem("s_x2T")
        s_hid = sem("s_hid"); s_silu = sem("s_silu"); s_lgp = sem("s_lgp"); s_lgs = sem("s_lgs")
        s_lst = [sem(f"s_lst{k}") for k in range(2)]
        s_lg = sem("s_lg")
        s_top = sem("s_top"); s_texp = sem("s_texp"); s_tpe = sem("s_tpe"); s_maps = sem("s_maps")
        s_bc = sem("s_bc"); s_tokens = sem("s_tokens"); s_hot = sem("s_hot"); s_x2h = sem("s_x2h"); s_x2l = sem("s_x2l")
        s_g = sem("s_g"); s_xgh = sem("s_xgh"); s_xgl = sem("s_xgl")
        s_ew = [sem(f"s_ew{j}") for j in range(EQ)]
        s_wh = sem("s_wh"); s_wl = sem("s_wl")
        s_gv0 = sem("s_gv0"); s_gv1 = sem("s_gv1"); s_sg0 = sem("s_sg0"); s_sg1 = sem("s_sg1")
        s_h0 = sem("s_h0"); s_h1 = sem("s_h1"); s_yp = sem("s_yp"); s_ys = sem("s_ys")
        s_perm = [sem(f"s_perm{k}") for k in range(2)]
        s_cold = sem("s_cold"); s_away = sem("s_away"); s_cold2 = sem("s_cold2"); s_c = sem("s_c"); s_y3 = sem("s_y3"); s_st3 = sem("s_st3")
        s_mv3 = sem("s_mv3"); s_ve3 = sem("s_ve3"); s_rstd3 = sem("s_rstd3"); s_fin = sem("s_fin")
        s_out = [sem(f"s_out{k}") for k in range(2)]

        def after(eng, s, n):
            if isinstance(n, int) and n < 0:
                return
            eng.wait_ge(s, n + 1)

        def live(n, count):
            return not isinstance(n, int) or 0 <= n < count

        def pipeline(eng, body, count, before, behind, turn=2):
            lo = 4
            hi = (count - before) // turn * turn
            for i in range(-before, lo):
                body(i, i // turn, i % turn)
            with eng.Fori(lo // turn, hi // turn) as h:
                for k in range(turn):
                    body(h * turn + k, h, k)
            for i in range(hi, count + behind):
                body(i, i // turn, i % turn)

        block = ctx.enter_context(nc.Block())

        @block.sync
        def _(sp):
            x_t = x.rearrange("b (t p) d -> b p t d", p=P)

            def fixed(n):
                return n if isinstance(n, int) else sp.snap(n)

            for h in range(H):
                sp.dma_start(om_raw[:, h, :], omega).then_inc(s_ld_feat, 16)
            sp.dma_start(wqk_raw[:, 0, :], Wq).then_inc(s_ld_feat, 16)
            sp.dma_start(wqk_raw[:, 1, :], Wk).then_inc(s_ld_feat, 16)
            sp.dma_start(xs[0][:], x_t[0]).then_inc(s_xs[0], 16)
            sp.dma_start(xs[1][:], x_t[1]).then_inc(s_xs[1], 16)
            for t in range(T):
                sp.dma_start(x_all[:, :, t * D:(t + 1) * D],
                             x[:, t * P:(t + 1) * P, :].rearrange("b p d -> p b d")).then_inc(s_x_all, 16)

            with sp.Fori(1, B // 2) as h:
                for k in range(2):
                    i, step = sp.snap(h * 2 + k), sp.snap(h * 2 + (k - 1))
                    sp.wait_ge(s_xt, step)
                    sp.dma_start(xs[k][:], x[ds(i, 1)].rearrange("b (t p) d -> p (b t) d", p=P)).then_inc(s_xs[k], 16)

            def load_expert(e, k):
                e = ds(fixed(e), 1)
                sp.dma_start(wgv[k][:, 0, :], w1[e].rearrange("e d f -> d (e f)")).then_inc(s_ew[k], 16)
                sp.dma_start(wgv[k][:, 1, :], w2[e].rearrange("e d f -> d (e f)")).then_inc(s_ew[k], 16)
                sp.dma_start(wdn[k][:], w3[e].rearrange("e (c p) d -> p (e c) d", p=P)).then_inc(s_ew[k], 16)

            def load_first():
                sp.wait_ge(s_lgs, B // 2)
                for j in range(EQ):
                    load_expert(j, j)

            with sp.Fori(0, B // 4) as h:
                for k in range(2):
                    for r in range(2):
                        b = sp.snap(h * 4 + (2 * k + r))
                        if r == 0:
                            done = sp.snap(h * 2 + (k + 1))
                            sp.wait_ge(s_lgs, done)
                        sp.dma_start(logits[ds(b, 1)].rearrange("b e s -> (b e) s"),
                                     lgs[k][:, r * S:(r + 1) * S]).then_inc(s_lst[k], 16)
            for k in range(2):
                sp.wait_ge(s_lst[k], 16 * 2 * (B // 4))
            for g in range(G):
                sp.dma_start(lg[:, g, :], logits[g * BG:(g + 1) * BG].rearrange("b e s -> (b e) s")).then_inc(s_lg, 16)
            load_first()

            def regroup(c, j):
                k = j % 2
                chunk, done = ds(fixed(c + 0), 1), fixed(c * EQ + (j + 1))
                sp.wait_ge(s_ys, done)
                for r in range(EQ):
                    sp.dma_start(y_all[CAP * j:CAP * (j + 1), chunk, :, r, :].rearrange("p c q d -> p (c q) d"),
                                 ys[k][CAP * r:CAP * (r + 1), :, :]).then_inc(s_perm[k], 16)

            with sp.Fori(0, CH - 1) as c:
                for j in range(EQ):
                    regroup(c, j)
                    load_expert(c * EQ + (j + EQ), j)
            for j in range(EQ):
                regroup(CH - 1, j)

            with sp.Fori(0, B // 2) as h:
                for k in range(2):
                    b, done = sp.snap(h * 2 + k), sp.snap(h * 2 + (k + 1))
                    sp.wait_ge(s_fin, done)
                    sp.dma_start(out[ds(b, 1)].rearrange("b (t p) d -> p (b t) d", p=P), outs[k][:]).then_inc(s_out[k], 16)
            for k in range(2):
                sp.wait_ge(s_out[k], 16 * (B // 2))

        @block.gpsimd
        def _(pool):
            pool.memset(ident[:], 0.0).then_inc(s_const, 1)
            pool.memset(mask[:], 1.0).then_inc(s_const, 1)
            pool.memset(minus_half[:], -0.5).then_inc(s_const, 1)
            pool.memset(inner_eps[:], INNER_EPS).then_inc(s_const, 1)
            pool.memset(ln_eps[:], LN_EPS).then_inc(s_const, 1)
            for k in range(2):
                pool.memset(vs[k][:, :, :, DH:DH + 1], 1.0).then_inc(s_const, 1)
            pool.iota(iota_i[:], pattern=[[1, S]], base=0, channel_multiplier=0).then_inc(s_const, 1)
            pool.iota(tok_i[:], pattern=[[P, T]], base=0, channel_multiplier=1).then_inc(s_const, 1)
            pool.wait_ge(s_const, 9)
            pool.affine_select(out=ident[:], in_=ident[:], compare_op=ALU.not_equal, fill=1.0,
                               base=0, pattern=[[-1, P]], channel_multiplier=1).then_inc(s_const, 1)
            pool.affine_select(out=mask[:], in_=mask[:], compare_op=ALU.is_ge, fill=0.0,
                               base=0, pattern=[[0, T * H], [1, P]], channel_multiplier=-1).then_inc(s_const, 1)

            pool.wait_ge(s_ld_w, 16 * N_LD_W)
            pool.wait_ge(s_x_all, 16 * T)

            def inv_std(i, s_var, s_eps, s_done, q, eps):
                after(pool, s_var, i)
                pool.tensor_tensor(ve[q][:], mv[q][:, :, 1], eps[:], ALU.add).then_inc(s_eps, 1)
                after(pool, s_eps, i)
                pool.tensor_tensor(rstd[q][:], ve[q][:], minus_half[:], ALU.pow).then_inc(s_done, 1)

            def layer(i, h, k):
                if live(i - 3, B):
                    n = i - 3
                    after(pool, s_x2, n)
                    pool.tensor_copy(x2_all[:, ds(n, 1), :],
                                     x2s[1 - k][:].rearrange("p t d -> p (t d)").unsqueeze(1)).then_inc(s_x2cp, 1)
                if live(i, B):
                    after(pool, s_y2, i - 2)
                    pool.tensor_tensor(resid[k][:].unsqueeze(1), x_all[:, ds(i, 1), :],
                                       b2r[:].rearrange("p t d -> p (t d)").unsqueeze(1), ALU.add).then_inc(s_resid, 1)
                if live(i, B):
                    after(pool, s_zhat, i - 1)
                    inv_std(i, s_mv, s_ve, s_rstd, 2, inner_eps)
                if live(i - 1, B):
                    after(pool, s_x2, i - 3)
                    inv_std(i - 1, s_mv2, s_ve2, s_rstd2, 1 - k, ln_eps)

            pipeline(pool, layer, B, 2, 3)

            def gather(i, h, k):
                if live(i, B):
                    after(pool, s_x2h, i)
                    after(pool, s_g, i - 2)
                    pool.tensor_tensor(x2l[k][:].rearrange("p t d -> p (t d)").unsqueeze(1), x2_all[:, ds(i, 1), :],
                                       x2h[k][:].bitcast(F32).rearrange("p t d -> p (t d)").unsqueeze(1),
                                       ALU.subtract).then_inc(s_x2l, 1)

            pipeline(pool, gather, B, 0, 0)

            def expert(e, h, j):
                if live(e, E):
                    after(pool, s_wh, e)
                    after(pool, s_gv1, e - 2)
                    pool.tensor_tensor(wl[j % 2][:], wgv[j][:], wh[j % 2][:].bitcast(F32), ALU.subtract).then_inc(s_wl, 1)

            pipeline(pool, expert, E, 0, 0, EQ)

            def scatter(i, h, k):
                if live(i, B):
                    after(pool, s_fin, i - 2)
                    inv_std(i, s_mv3, s_ve3, s_rstd3, k, ln_eps)

            pipeline(pool, scatter, B, 0, 0)

        @block.scalar
        def _(act):
            act.dma_start(wv[:], Wv).then_inc(s_ld_w, 16)
            act.dma_start(wo[:], Wo).then_inc(s_ld_w, 16)
            act.dma_start(wf1[:], W1).then_inc(s_ld_w, 16)
            act.dma_start(wf2[:], W2.rearrange("(c p) d -> p c d", p=P)).then_inc(s_ld_w, 16)
            with nc.allow_non_contiguous_dma(reason="bias and scale vectors as columns"):
                act.dma_start(b1c[:], b1.rearrange("(c p) -> p c", p=P)).then_inc(s_ld_w, 16)
                act.dma_start(gam[:], gamma.rearrange("(p a) -> p a", a=1)).then_inc(s_ld_w, 16)
                act.dma_start(bet[:], beta.rearrange("(p a) -> p a", a=1)).then_inc(s_ld_w, 16)
            for t in range(T):
                act.dma_start(b2r[:, t, :], b2.rearrange("(a d) -> a d", a=1).to_broadcast([P, D])).then_inc(s_ld_w, 16)
            act.dma_start(rw1[:], router_w1).then_inc(s_ld_r, 16)
            act.dma_start(rw2[:], router_w2).then_inc(s_ld_r, 16)

            act.wait_ge(s_ld_w, 16 * N_LD_W)

            def exps(i, t):
                for f in range(NF):
                    n = t * NF + f
                    op = act.activation(feat[:, n, :], ps(t)[:, f * M:(f + 1) * M], ACT.Exp, bias=negmax[:, n:n + 1])
                if t == T - 1:
                    op.then_inc(s_exp, 1)

            def layer(i, h, k):
                if live(i, B):
                    after(act, s_ft0, i)
                    act.activation(featT[:, 0:H, :].rearrange("p f s -> p (f s)"), ps(2), ACT.Copy, bias=FEAT_EPS, scale=FEAT_SCALE)
                    after(act, s_ft1, i)
                    act.activation(featT[:, H:, :].rearrange("p f s -> p (f s)"), ps(3), ACT.Copy, bias=FEAT_EPS,
                                   scale=FEAT_SCALE).then_inc(s_feat, 1)
                if live(i - 3, B):
                    after(act, s_x2t, i - 3)
                    act.activation(x2T_all[:, ds(i - 3, 1), :], ps(5)[:, 0:S].unsqueeze(1), ACT.Copy).then_inc(s_x2T, 1)
                if live(i + 1, B):
                    after(act, s_v, i + 1)
                    act.activation(vs[1 - k][:, :, :, 0:DH], ps(6)[:, 0:T * D].rearrange("p (t h d) -> p t h d", t=T, h=H),
                                   ACT.Copy).then_inc(s_vs, 1)
                if live(i - 1, B):
                    after(act, s_zt, i - 1)
                    act.activation(hT[:], ps(7)[:, 0:S], ACT.Identity, bias=bet[:], scale=gam[:]).then_inc(s_hT, 1)
                if live(i + 1, B):
                    after(act, s_negmax, i + 1)
                    exps(i + 1, 0)
                if live(i, B):
                    after(act, s_sc, i)
                    act.activation(cross[:].rearrange("p h s -> p (h s)"), ps(5)[:, 0:H * P], ACT.Copy).then_inc(s_cross, 1)
                if live(i + 1, B):
                    exps(i + 1, 1)
                if live(i - 1, B):
                    for c in range(FC):
                        if c % 2 == 0:
                            after(act, (s_f1a, s_f1b)[c // 2], i - 1)
                        op = act.activation(reluT[:, c, :], ps(2 + c // 2)[:, c % 2 * S:(c % 2 + 1) * S], ACT.Relu,
                                            bias=b1c[:, c:c + 1])
                    op.then_inc(s_relu, 1)
                if live(i, B):
                    after(act, s_at, i)
                    act.activation(attnT[:], ps(5)[:, 0:S], ACT.Copy).then_inc(s_attnT, 1)
                if live(i + 2, B):
                    after(act, s_xt, i + 2)
                    act.activation(xT[:], ps(0)[:, 0:S], ACT.Copy).then_inc(s_xT, 1)

            pipeline(act, layer, B, 2, 3)

            def router(q, h, k):
                if live(q, B // 2):
                    after(act, s_hid, q)
                    act.activation(silu[k][:], ps(k), ACT.Silu).then_inc(s_silu, 1)

            pipeline(act, router, B // 2, 0, 0)

            act.wait_ge(s_top, 1)
            for g in range(G):
                act.activation(lg[:, g, :], lg[:, g, :], ACT.Exp, bias=nmx[:, g:g + 1],
                               accum_out=ssum[:, g:g + 1]).then_inc(s_texp, 1)

            def gather(i, h, k):
                if live(i, B):
                    after(act, s_g, i - 2)
                    act.activation(x2h[k][:].rearrange("p t d -> p (t d)").unsqueeze(1), x2_all[:, ds(i, 1), :],
                                   ACT.Copy).then_inc(s_x2h, 1)
                    after(act, s_bc, i)
                    after(act, s_hot, i - 2)
                    act.activation(tokens[k][:], ps(k), ACT.Copy).then_inc(s_tokens, 1)
                if live(i - 1, B):
                    after(act, s_g, i - 1)
                    act.activation(xgh[:, :, ds(i - 1, 1), :].rearrange("p e b c -> p (e b) c"),
                                   ps(3 - k).rearrange("p (e c) -> p e c", e=E), ACT.Copy).then_inc(s_xgh, 1)

            act.wait_ge(s_x2cp, B)
            pipeline(act, gather, B, 0, 1)

            def expert(e, h, j):
                k = j % 2
                if live(e, E):
                    act.wait_ge(s_ew[j], 48 * (h + 1) if isinstance(e, int) else h * 48 + 48)
                    after(act, s_gv1, e - 2)
                    act.activation(wh[k][:], wgv[j][:], ACT.Copy).then_inc(s_wh, 1)
                if live(e - 1, E):
                    after(act, s_gv0, e - 1)
                    after(act, s_h0, e - 2)
                    act.activation(sg[:, 0, :], ps(0), ACT.Silu).then_inc(s_sg0, 1)
                if live(e - 2, E):
                    after(act, s_yp, e - 2)
                    if not isinstance(e, int) or e >= 4:
                        act.wait_ge(s_perm[k], h * (32 * EQ) + (j // 2 - 1) * (16 * EQ))
                    act.activation(ys[k][:].rearrange("p q d -> p (q d)"), ps(4 + k), ACT.Copy).then_inc(s_ys, 1)
                if live(e - 1, E):
                    after(act, s_gv1, e - 1)
                    after(act, s_h1, e - 2)
                    act.activation(sg[:, 1, :], ps(2), ACT.Silu).then_inc(s_sg1, 1)

            pipeline(act, expert, E, 0, 2, EQ)

            def scatter(i, h, k):
                if live(i, B):
                    after(act, s_c, i - 2)
                    for c in range(CH // 2):
                        op = act.activation(away[k][:, c, :], iota[:], ACT.Abs, bias=minus_tok[:, ds(i * CH + (CH // 2 + c), 1)])
                    op.then_inc(s_away, 1)
                    after(act, s_away, i)
                    for c in range(CH // 2):
                        col = ds(i * CH + (CH // 2 + c), 1)
                        op = act.activation(cold[k][:, CH // 2 + c, :], away[k][:, c, :], ACT.Relu, bias=slot_w[:, col],
                                            scale=minus_w[:, col])
                    op.then_inc(s_cold2, 1)

            pipeline(act, scatter, B, 0, 0)

        @block.vector
        def _(dve):
            dve.wait_ge(s_const, 11)
            dve.tensor_reduce(m4[:], ident[:].rearrange("p (q j) -> p j q", j=EQ), AX.X, ALU.add).then_inc(s_sel, 1)
            dve.tensor_reduce(r32[:], ident[:].rearrange("p (q j) -> p q j", j=EQ), AX.X, ALU.add).then_inc(s_sel, 1)
            dve.tensor_reduce(m16[:], ident[:].rearrange("p (b e) -> p e b", e=E), AX.X, ALU.add).then_inc(s_sel, 1)
            dve.tensor_reduce(b8[:], ident[:].rearrange("p (b e) -> p b e", e=E), AX.X, ALU.add).then_inc(s_sel, 1)
            dve.tensor_copy(iota[:], iota_i[:]).then_inc(s_sel, 1)
            dve.tensor_copy(tok[:], tok_i[:]).then_inc(s_sel, 1)
            dve.wait_ge(s_sel, 4)
            for g in range(G):
                dve.tensor_copy(lb[:, g * BG:(g + 1) * BG, :], b8[:].unsqueeze(2).to_broadcast([P, BG, P])).then_inc(s_sel, 1)

            dve.wait_ge(s_prep_pe, 1)
            dve.tensor_copy(wqkT[:].rearrange("p n d -> p (n d)"), ps(0)[:, 0:2 * D]).then_inc(s_prep_ev, 1)
            dve.tensor_copy(omT[:], ps(0)[:, 2 * D:2 * D + M]).then_inc(s_prep_ev, 1)
            dve.wait_ge(s_prep_pe, 2)
            for h in range(H):
                dve.tensor_scalar(wfeat[:].rearrange("p (n h m) -> p n h m", n=2, h=H)[:, :, h, :],
                                  ps(1 + h)[:, 0:2 * M].rearrange("p (n m) -> p n m", n=2), SCALE, None,
                                  ALU.mult).then_inc(s_prep_ev, 1)

            dve.wait_ge(s_ld_w, 16 * N_LD_W)
            dve.wait_ge(s_x_all, 16 * T)

            def sums(src, q, s_stats):
                for t in range(T):
                    op = dve.bn_stats(stats[q][:, t, :], src[:, t, :])
                op.then_inc(s_stats, 1)

            def moments(sums_at, q, s_done):
                for t in range(T):
                    op = dve.bn_aggr(mv[q][:, t, :], stats[sums_at][:, t, :])
                op.then_inc(s_done, 1)

            def normalise(dst, src, q, s_done):
                for t in range(T):
                    op = dve.tensor_scalar(dst[:, t, :], src[:, t, :], mv[q][:, t, 0:1], rstd[q][:, t:t + 1],
                                           ALU.subtract, ALU.mult)
                op.then_inc(s_done, 1)

            def layer(i, h, k):
                if live(i + 1, B):
                    after(dve, s_proj0, i + 1)
                    dve.tensor_reduce(negmax[:, 0:NF], ps(0).rearrange("p (f m) -> p f m", f=NF), AX.X, ALU.max,
                                      negate=True)
                    after(dve, s_proj1, i + 1)
                    dve.tensor_reduce(negmax[:, NF:], ps(1).rearrange("p (f m) -> p f m", f=NF), AX.X, ALU.max,
                                      negate=True).then_inc(s_negmax, 1)
                if live(i, B):
                    after(dve, s_sc, i)
                    dve.tensor_tensor(diag[:].rearrange("p n s -> p (n s)"), ps(4), mask[:].rearrange("p n s -> p (n s)"),
                                      ALU.mult).then_inc(s_diag, 1)
                if live(i, B):
                    after(dve, s_av, i)
                    av = ps(4)[:, 0:T * H * (DH + 1)].rearrange("p (g d) -> p g d", d=DH + 1)
                    dve.tensor_scalar(den[:].unsqueeze(2), av[:, :, DH:DH + 1], FEAT_EPS, None, ALU.add).then_inc(s_den, 1)
                    after(dve, s_den, i)
                    dve.reciprocal(rden[:], den[:]).then_inc(s_rden, 1)
                    after(dve, s_rden, i)
                    dve.tensor_tensor(attn[:], av[:, :, 0:DH], rden[:].unsqueeze(2).to_broadcast([P, T * H, DH]),
                                      ALU.mult).then_inc(s_attn, 1)
                if live(i - 1, B):
                    after(dve, s_f2, i - 1)
                    after(dve, s_resid, i - 1)
                    after(dve, s_x2, i - 3)
                    dve.tensor_tensor(y2[1 - k][:].rearrange("p t d -> p (t d)"), ps(7)[:, 0:S], resid[1 - k][:],
                                      ALU.add).then_inc(s_y2, 1)
                    after(dve, s_y2, i - 1)
                    sums(y2[1 - k], 0, s_st2)
                if live(i, B):
                    after(dve, s_wo, i)
                    dve.tensor_tensor(y[:].rearrange("p t d -> p (t d)").unsqueeze(1), ps(6)[:, 0:S].unsqueeze(1),
                                      x_all[:, ds(i, 1), :], ALU.add).then_inc(s_y, 1)
                    after(dve, s_y, i)
                    sums(y, 1, s_st)
                if live(i - 1, B):
                    after(dve, s_st2, i - 1)
                if live(i, B):
                    after(dve, s_st, i)
                if live(i - 2, B):
                    after(dve, s_rstd2, i - 2)
                    after(dve, s_x2t, i - 4)
                    after(dve, s_x2cp, i - 4)
                    normalise(x2s[k], y2[k], k, s_x2)
                if live(i, B):
                    moments(1, 2, s_mv)
                if live(i - 1, B):
                    moments(0, 1 - k, s_mv2)
                if live(i, B):
                    after(dve, s_rstd, i)
                    normalise(zhat, y, 2, s_zhat)

            pipeline(dve, layer, B, 2, 2)

            def router(q, h, k):
                if live(q - 1, B // 2):
                    after(dve, s_lgp, q - 1)
                    stored(dve, q - 1, h if k else h - 1, 1 - k)
                    dve.tensor_copy(lgs[1 - k][:], ps(3 - k)[0:E, :]).then_inc(s_lgs, 1)

            def stored(eng, q, turn, k):
                if isinstance(q, int) and q < 2:
                    return
                eng.wait_ge(s_lst[k], turn * 32)

            pipeline(dve, router, B // 2, 0, 1)

            dve.wait_ge(s_lg, 16 * G)
            dve.tensor_reduce(nmx[:], lg[:], AX.X, ALU.max, negate=True).then_inc(s_top, 1)
            dve.wait_ge(s_texp, G)
            done = 1

            def step(ins):
                nonlocal done
                done += 1
                ins.then_inc(s_top, 1)
                dve.wait_ge(s_top, done)

            step(dve.reciprocal(rsum[:], ssum[:]))
            step(dve.tensor_tensor(lg[:], lg[:], rsum[:].unsqueeze(2).to_broadcast([P, G, S]), ALU.mult))
            for r in range(CAP // 8):
                for g in range(G):
                    top = val[:, g, 8 * r:8 * r + 8]
                    step(dve.max(top, lg[:, g, :]))
                    step(dve.max_index(idx[:, g, 8 * r:8 * r + 8], top, lg[:, g, :]))
                    if r < CAP // 8 - 1:
                        step(dve.match_replace(lg[:, g, :], top, lg[:, g, :], -1.0))
            step(dve.tensor_reduce(wsum[:], val[:], AX.X, ALU.add))
            step(dve.tensor_scalar(wsum[:], wsum[:], WEIGHT_EPS, None, ALU.add))
            step(dve.reciprocal(wrec[:], wsum[:]))
            step(dve.tensor_tensor(wgt[:], val[:], wrec[:].unsqueeze(2).to_broadcast([P, G, CAP]), ALU.mult))
            step(dve.tensor_copy(idxf[:], idx[:]))
            for g in range(G):
                dve.tensor_tensor(r3[:, g], idxf[:, g].unsqueeze(1).to_broadcast([P, E, CAP]),
                                  m16[:].unsqueeze(2).to_broadcast([P, E, CAP]), ALU.mult)
                dve.tensor_tensor(idx4[:, g], idxf[:, g].unsqueeze(1).to_broadcast([P, EQ, CAP]),
                                  m4[:].unsqueeze(2).to_broadcast([P, EQ, CAP]), ALU.mult)
                op = dve.tensor_tensor(wgt4[:, g], wgt[:, g].unsqueeze(1).to_broadcast([P, EQ, CAP]),
                                       m4[:].unsqueeze(2).to_broadcast([P, EQ, CAP]), ALU.mult)
            op.then_inc(s_tpe, 1)
            dve.wait_ge(s_tpe, 2)
            half = B * CH
            dve.tensor_copy(slot_tok[:], ps(0)[:, 0:half]).then_inc(s_maps, 1)
            dve.tensor_copy(slot_w[:], ps(1)[:, 0:half]).then_inc(s_maps, 1)
            dve.tensor_scalar(minus_tok[:], ps(0)[:, 0:half], -1.0, None, ALU.mult).then_inc(s_maps, 1)
            dve.tensor_scalar(minus_w[:], ps(1)[:, 0:half], -1.0, None, ALU.mult).then_inc(s_maps, 1)

            def gather(i, h, k):
                if live(i, B):
                    after(dve, s_tokens, i)
                    after(dve, s_g, i - 2)
                    for t in range(T):
                        op = dve.tensor_scalar(hot[k][:, t, :], tokens[k][:], tok[:, t:t + 1], None, ALU.is_equal)
                    op.then_inc(s_hot, 1)
                if live(i - 1, B):
                    after(dve, s_xgh, i - 1)
                    row = ds(i - 1, 1)
                    dve.tensor_tensor(xgl[:, :, row, :].rearrange("p e b c -> p (e b) c"),
                                      ps(3 - k).rearrange("p (e c) -> p e c", e=E),
                                      xgh[:, :, row, :].rearrange("p e b c -> p (e b) c").bitcast(F32),
                                      ALU.subtract).then_inc(s_xgl, 1)

            pipeline(dve, gather, B, 0, 1)

            def expert(e, h, j):
                k = j % 2
                if live(e, E):
                    after(dve, s_yp, e - 2)
                    after(dve, s_sg0, e)
                    dve.tensor_tensor(hm[k][:, 0, :], sg[:, 0, :], ps(1), ALU.mult).then_inc(s_h0, 1)
                    after(dve, s_sg1, e)
                    dve.tensor_tensor(hm[k][:, 1, :], sg[:, 1, :], ps(3), ALU.mult).then_inc(s_h1, 1)

            pipeline(dve, expert, E, 0, 0, EQ)

            def cold_maps(i, k):
                after(dve, s_c, i - 2)
                for c in range(CH // 2):
                    col = ds(i * CH + c, 1)
                    op = dve.tensor_scalar(cold[k][:, c, :], iota[:], slot_tok[:, col], slot_w[:, col],
                                           ALU.is_equal, ALU.mult)
                op.then_inc(s_cold, 1)

            def scatter(i, h, k):
                if live(i + 1, B):
                    cold_maps(i + 1, 1 - k)
                if live(i, B):
                    after(dve, s_c, i)
                    after(dve, s_fin, i - 2)
                    dve.tensor_tensor(y3[k][:].rearrange("p t d -> p (t d)").unsqueeze(1), ps(k)[:, 0:S].unsqueeze(1),
                                      x2_all[:, ds(i, 1), :], ALU.add).then_inc(s_y3, 1)
                    after(dve, s_y3, i)
                    sums(y3[k], k, s_st3)
                    after(dve, s_st3, i)
                if live(i - 1, B):
                    after(dve, s_rstd3, i - 1)
                    if not isinstance(i, int) or i >= 3:
                        dve.wait_ge(s_out[1 - k], (h * 16 if k else h * 16 - 16))
                    normalise(outs[1 - k], y3[1 - k], 1 - k, s_fin)
                if live(i, B):
                    moments(k, k, s_mv3)

            pipeline(dve, scatter, B, 1, 1)

        @block.tensor
        def _(pe):
            pe.wait_ge(s_const, 11)
            pe.wait_ge(s_ld_feat, 16 * (2 + H))
            for n in range(2):
                pe.transpose(ps(0)[:, n * D:(n + 1) * D], wqk_raw[:, n, :], ident[:])
            pe.transpose(ps(0)[:, 2 * D:2 * D + M], om_raw[:].rearrange("p h d -> p (h d)"), ident[:]).then_inc(s_prep_pe, 1)
            pe.wait_ge(s_prep_ev, 2)
            for n in range(2):
                for h in range(H):
                    op = pe.matmul(ps(1 + h)[:, n * M:(n + 1) * M], wqkT[h * DH:(h + 1) * DH, n, :],
                                   omT[h * DH:(h + 1) * DH, :], start=True, stop=True)
            op.then_inc(s_prep_pe, 1)

            def transposes(dst, src, s):
                for t in range(T):
                    op = pe.transpose(dst[:, t * P:(t + 1) * P], src[:, t, :], ident[:])
                op.then_inc(s, 1)

            def features(i):
                after(pe, s_exp, i)
                for f in range(NF):
                    for t in range(T):
                        op = pe.transpose(ps(2 + f // 2)[:, f % 2 * S + t * P:f % 2 * S + (t + 1) * P],
                                          feat[:, t * NF + f, :], ident[:])
                    if f % 2:
                        op.then_inc((s_ft0, s_ft1)[f // 2], 1)

            def project(i):
                after(pe, s_xT, i)
                for t in range(T):
                    pe.matmul(ps(t), xT[:, t * P:(t + 1) * P], wfeat[:], start=True, stop=True)\
                      .then_inc((s_proj0, s_proj1)[t], 1)
                after(pe, s_y, i - 2)
                for t in range(T):
                    op = pe.matmul(ps(6)[:, t * D:(t + 1) * D], xT[:, t * P:(t + 1) * P], wv[:], start=True, stop=True)
                op.then_inc(s_v, 1)

            def qk(i):
                after(pe, s_feat, i)
                after(pe, s_x2T, i - 3)
                for h in range(H):
                    q, kf = featT[:, h, :], featT[:, H + h, :]
                    for t in range(T):
                        tile = slice(t * P, (t + 1) * P)
                        pe.matmul(ps(4)[:, (h * T + t) * P:(h * T + t + 1) * P], kf[:, tile], q[:, tile], start=True, stop=True)
                    op = pe.matmul(ps(5)[:, h * P:(h + 1) * P], kf[:, 0:P], q[:, P:S], start=True, stop=True)
                op.then_inc(s_sc, 1)

            def attend(i, k):
                after(pe, s_diag, i)
                after(pe, s_cross, i)
                after(pe, s_vs, i)
                w = DH + 1
                for h in range(H):
                    pe.matmul(ps(4)[:, h * w:(h + 1) * w], diag[:, h * T, :], vs[k][:, 0, h, :], start=True, stop=True)
                    to = ps(4)[:, (H + h) * w:(H + h + 1) * w]
                    pe.matmul(to, cross[:, h, :], vs[k][:, 0, h, :], start=True, stop=False)
                    op = pe.matmul(to, diag[:, h * T + 1, :], vs[k][:, 1, h, :], start=False, stop=True)
                op.then_inc(s_av, 1)

            def ffn_up(i):
                after(pe, s_hT, i)
                for c in range(FC):
                    op = pe.matmul(ps(2 + c // 2)[:, c % 2 * S:(c % 2 + 1) * S], wf1[:, c * P:(c + 1) * P], hT[:],
                                   start=True, stop=True)
                    if c % 2:
                        op.then_inc((s_f1a, s_f1b)[c // 2], 1)

            def ffn_down(i, t):
                for c in range(FC):
                    op = pe.matmul(ps(7)[:, t * D:(t + 1) * D], reluT[:, c, t * P:(t + 1) * P], wf2[:, c, :],
                                   start=(c == 0), stop=(c == FC - 1))
                if t == T - 1:
                    op.then_inc(s_f2, 1)

            def layer(i, h, k):
                if live(i, B):
                    features(i)
                if live(i - 3, B):
                    after(pe, s_x2, i - 3)
                    if not live(i - 1, B):
                        after(pe, s_x2T, i - 4)
                    transposes(ps(5), x2s[1 - k], s_x2t)
                if live(i + 1, B):
                    project(i + 1)
                if live(i - 1, B):
                    after(pe, s_zhat, i - 1)
                    after(pe, s_y2, i - 2)
                    transposes(ps(7), zhat, s_zt)
                if live(i, B):
                    qk(i)
                if live(i - 1, B):
                    ffn_up(i - 1)
                if live(i, B):
                    attend(i, k)
                if live(i - 1, B):
                    after(pe, s_relu, i - 1)
                    ffn_down(i - 1, 0)
                if live(i, B):
                    after(pe, s_attn, i)
                    transposes(ps(5), attn[:].rearrange("p (t h) d -> p t (h d)", t=T), s_at)
                if live(i - 1, B):
                    ffn_down(i - 1, 1)
                if live(i, B):
                    after(pe, s_attnT, i)
                    if live(i + 1, B):
                        after(pe, s_vs, i + 1)
                    for t in range(T):
                        op = pe.matmul(ps(6)[:, t * D:(t + 1) * D], attnT[:, t * P:(t + 1) * P], wo[:],
                                       start=True, stop=True)
                    op.then_inc(s_wo, 1)
                if live(i + 2, B):
                    if isinstance(i, int):
                        pe.wait_ge(s_xs[k], 16 * (h + 2))
                    else:
                        pe.wait_ge(s_xs[k], h * 16 + 32)
                    if live(i + 1, B):
                        after(pe, s_exp, i + 1)
                    transposes(ps(0), xs[k], s_xt)

            pe.wait_ge(s_prep_ev, 2 + H)
            pe.wait_ge(s_ld_w, 16 * N_LD_W)
            pipeline(pe, layer, B, 2, 3)

            def router(q, h, k):
                if live(q + 1, B // 2):
                    after(pe, s_silu, q - 1)
                    n = q + 1
                    src = x2T_all[:, ds(2 * n if isinstance(n, int) else n * 2, 2), :]
                    pe.matmul(ps(1 - k), rw1[:], src, start=True, stop=True).then_inc(s_hid, 1)
                if live(q, B // 2):
                    after(pe, s_silu, q)
                    after(pe, s_lgs, q - 2)
                    pe.matmul(ps(2 + k)[0:E, :], rw2[:], silu[k][:], start=True, stop=True).then_inc(s_lgp, 1)

            pe.wait_ge(s_ld_r, 32)
            pe.wait_ge(s_x2T, B)
            pipeline(pe, router, B // 2, 1, 0)

            pe.wait_ge(s_tpe, 1)
            for g in range(G):
                cols = slice(g * P // EQ, (g + 1) * P // EQ)
                pe.matmul(ps(0)[:, cols], idx4[:, g].rearrange("p j c -> p (j c)"), r32[:], start=True, stop=True)
                op = pe.matmul(ps(1)[:, cols], wgt4[:, g].rearrange("p j c -> p (j c)"), r32[:], start=True, stop=True)
            op.then_inc(s_tpe, 1)
            pe.wait_ge(s_maps, 4)

            def gather(i, h, k):
                if live(i + 1, B):
                    n = i + 1
                    after(pe, s_tokens, i - 1)
                    g = n // BG
                    pe.matmul(ps(1 - k), lb[:, ds(n, 1), :].rearrange("p a m -> p (a m)"),
                              r3[:, ds(g, 1)].rearrange("p a e c -> p (a e c)"), start=True, stop=True).then_inc(s_bc, 1)
                if live(i, B):
                    after(pe, s_hot, i)
                    after(pe, s_x2l, i)
                    after(pe, s_xgl, i - 2)
                    for t in range(T):
                        for part in (x2l, x2h):
                            op = pe.matmul(ps(2 + k), part[k][:, t, :], hot[k][:, t, :],
                                           start=(t == 0 and part is x2l), stop=(t == T - 1 and part is x2h))
                    op.then_inc(s_g, 1)

            pipeline(pe, gather, B, 1, 0)

            def expert(e, h, j):
                k = j % 2

                def gate_value(c, s):
                    xh, xl = (x[:, ds(e, 1)].rearrange("p a b c -> p (a b c)") for x in (xgh, xgl))
                    for n in range(2):
                        wide = slice(c * P, (c + 1) * P)
                        to = ps(2 * c + n)
                        pe.matmul(to, wl[k][:, n, wide], xh, start=True, stop=False)
                        pe.matmul(to, wh[k][:, n, wide], xl, start=False, stop=False)
                        op = pe.matmul(to, wh[k][:, n, wide], xh, start=False, stop=True)
                    op.then_inc(s, 1)

                if live(e, E):
                    after(pe, s_wl, e)
                    after(pe, s_h0, e - 1)
                    gate_value(0, s_gv0)
                if live(e - 1, E):
                    after(pe, s_h1, e - 1)
                    after(pe, s_ys, e - 3)
                    for q in range(B // EQ):
                        for c in range(EC):
                            op = pe.matmul(ps(5 - k)[:, q * D:(q + 1) * D], hm[1 - k][:, c, q * P:(q + 1) * P],
                                           wdn[(j - 1) % EQ][:, c, :], start=(c == 0), stop=(c == EC - 1))
                    op.then_inc(s_yp, 1)
                if live(e, E):
                    gate_value(1, s_gv1)

            pe.wait_ge(s_xgl, B)
            pipeline(pe, expert, E, 0, 1, EQ)

            def scatter(i, h, k):
                if live(i, B):
                    after(pe, s_cold, i)
                    after(pe, s_cold2, i)
                    after(pe, s_y3, i - 2)
                    for t in range(T):
                        for c in range(CH):
                            src = y_flat[:, c, ds(i, 1), :].rearrange("p a d -> p (a d)")
                            op = pe.matmul(ps(k)[:, t * D:(t + 1) * D], cold[k][:, c, t * P:(t + 1) * P], src,
                                           start=(c == 0), stop=(c == CH - 1))
                    op.then_inc(s_c, 1)

            y_flat = y_all[:].rearrange("p c q r d -> p c (q r) d")
            for k in range(2):
                pe.wait_ge(s_perm[k], 16 * EQ * (E // 2))
            pipeline(pe, scatter, B, 0, 0)


_INS = ['L0_attn_batch', 'L0_attn_Wq', 'L0_attn_Wk', 'L0_attn_Wv', 'L0_attn_Wo', 'L0_attn_omega', 'L0_attn_W1',
        'L0_attn_b1', 'L0_attn_W2', 'L0_attn_b2', 'L0_attn_gamma', 'L0_attn_beta', 'L0_ffn_router_w1',
        'L0_ffn_router_w2', 'L0_ffn_w1', 'L0_ffn_w2', 'L0_ffn_w3']


def kernel(**inputs):
    import numpy as _np
    import concourse.bacc as _bacc
    from concourse import mybir as _mybir
    from concourse.bass_utils import run_bass_kernel_spmd as _run

    nc = _bacc.Bacc("TRN2", target_bir_lowering=False, num_devices=1)
    arrays, args = {}, []
    for name in _INS:
        a = _np.ascontiguousarray(inputs[name])
        arrays[f"in_{name}_dram"] = a
        args.append(nc.dram_tensor(f"in_{name}_dram", a.shape, _mybir.dt.from_np(a.dtype), kind="ExternalInput").ap())
    shape = inputs['L0_attn_batch'].shape
    experts = inputs['L0_ffn_w1'].shape[0]
    logits = nc.dram_tensor("router_logits", (shape[0], experts, shape[1]), _mybir.dt.float32, kind="Internal").ap()
    res = nc.dram_tensor("out_0_dram", shape, _mybir.dt.float32, kind="ExternalOutput").ap()
    post_ln_block(nc, *args, logits, res)
    r = _run(nc, [arrays], core_ids=[0])
    return r.results[0]["out_0_dram"]
```

```python
from contextlib import ExitStack

import concourse.bass as bass
from concourse import mybir

ALU = mybir.AluOpType
ACT = mybir.ActivationFunctionType
AX = mybir.AxisListType
F32 = mybir.dt.float32
F32R = mybir.dt.float32r
BF16 = mybir.dt.bfloat16
I32 = mybir.dt.int32
U32 = mybir.dt.uint32
ds = bass.ds

P = 128
INNER_EPS = 1e6
FEAT_EPS = 1e-6
LN_EPS = 1e-5
WEIGHT_EPS = 1e-9
EXP_MAX = 1e38


def post_ln_block(nc, x, Wq, Wk, Wv, Wo, omega, W1, b1, W2, b2, gamma, beta,
                  router_w1, router_w2, w1, w2, w3, out):
    B, S, D = x.shape
    M, DH = omega.shape
    H = D // DH
    FF = W1.shape[1]
    FC = FF // P
    E, _, EF = w1.shape
    EC = EF // P
    HID = router_w1.shape[1]
    T = S // P
    CAP = 2 * S // E
    G = B * E // P
    BG = B // G
    EQ = P // CAP
    CH = E // EQ
    SLOTS = E * CAP
    ES = B * CAP
    NP = 3
    NF = 2 * H
    assert D == P and M == P and T == 2 and H == 2 and S == 256 and HID == P
    assert SLOTS == 512 and ES == 512 and B % 2 == 0 and E % EQ == 0 and G == 2
    SCALE = float(DH) ** -0.25
    FEAT_SCALE = float(M) ** -0.5

    with ExitStack() as ctx:
        early = ctx.enter_context(ExitStack())

        def sb(name, shape, dt=F32, stack=ctx):
            return stack.enter_context(nc.sbuf_tensor(name, shape, dt))

        def eb(name, shape, dt=F32):
            return sb(name, shape, dt, early)

        def sem(name):
            return ctx.enter_context(nc.semaphore(name))

        bank = [ctx.enter_context(nc.psum_tensor(f"bank{n}", [P, 2, 512], F32)) for n in range(4)]

        def ps(n):
            return bank[n // 2][:, n % 2, :]

        ident = sb("ident", [P, P])
        minus_half = sb("minus_half", [P, T])
        inner_eps = sb("inner_eps", [P, T])
        ln_eps = sb("ln_eps", [P, T])
        silu_in = sb("silu_in", [P, T])
        iota_i = sb("iota_i", [P, S], I32)
        iota = sb("iota", [P, S])
        tok_i = sb("tok_i", [P, T], I32)
        tok = sb("tok", [P, T])
        m4 = sb("m4", [P, EQ])
        q4 = sb("q4", [P, EQ])
        m16 = sb("m16", [P, E])
        r32 = sb("r32", [P, P // EQ])
        re = sb("re", [P, P // EQ])
        b8 = sb("b8", [P, BG])
        lb = sb("lb", [P, B, P], BF16)

        x2_all = sb("x2_all", [P, B, S])
        mv = [sb(f"mv{k}", [P, T, 2]) for k in range(4)]
        ve = [sb(f"ve{k}", [P, T]) for k in range(4)]
        rstd = [sb(f"rstd{k}", [P, T]) for k in range(4)]
        stats = [sb(f"stats{k}", [P, T, 6]) for k in range(2)]

        lg = sb("lg", [P, G, S])
        nmx = sb("nmx", [P, G])
        ssum = sb("ssum", [P, G])
        rsum = sb("rsum", [P, G])
        val = sb("val", [P, G, CAP])
        idx = sb("idx", [P, G, CAP], U32)
        idxf = sb("idxf", [P, G, CAP])
        wsum = sb("wsum", [P, G])
        wrec = sb("wrec", [P, G])
        wgt = sb("wgt", [P, G, CAP])
        idx4 = sb("idx4", [P, G, EQ, CAP])
        wgt4 = sb("wgt4", [P, G, EQ, CAP])
        r3 = sb("r3", [P, G, E, CAP], BF16)
        slot_tok = sb("slot_tok", [P, B * CH])
        slot_w = sb("slot_w", [P, B // EQ, E])

        wgv = [sb(f"wgv{m}", [P, 2, 2, EF]) for m in range(2)]
        wdn = [sb(f"wdn{m}", [P, 2, EC, D]) for m in range(2)]

        lgs = [sb(f"lgs{k}", [E, S]) for k in range(2)]

        mask = eb("mask", [P, T * H, P])
        w_raw = eb("w_raw", [P, 3, D])
        wT = eb("wT", [P, 3, D])
        om_raw = eb("om_raw", [P, H, DH])
        omT = eb("omT", [P, M])
        wo = eb("wo", [P, D])
        wfeat_h = eb("wfeat_h", [P, NF * M], F32R)
        wfeat_l = eb("wfeat_l", [P, NF * M], F32R)
        wvo_h = eb("wvo_h", [P, H * D], F32R)
        wvo_l = eb("wvo_l", [P, H * D], F32R)
        wf1 = eb("wf1", [P, FF])
        wf1_h = eb("wf1_h", [P, FF], F32R)
        wf1_l = eb("wf1_l", [P, FF], F32R)
        wf2 = eb("wf2", [P, FC, D])
        b1c = eb("b1c", [P, FC])
        b1s = eb("b1s", [P, FC])
        b2r = eb("b2r", [P, T, D])
        gam = eb("gam", [P, 1])
        bet = eb("bet", [P, 1])
        x_all = eb("x_all", [P, B, S])
        xs = [eb(f"xs{k}", [P, T, D]) for k in range(2)]
        xT_h = eb("xT_h", [P, S], F32R)
        xT_l = eb("xT_l", [P, S], F32R)
        vs = [eb(f"vs{k}", [P, T, H, D + 1]) for k in range(2)]
        negmax = eb("negmax", [P, T * NF])
        feat = eb("feat", [P, T * NF, M])
        featT = eb("featT", [P, NF, S])
        diag = eb("diag", [P, H * T, P])
        cross = eb("cross", [P, H, P])
        den = eb("den", [P, T, H])
        rden = eb("rden", [P, T, H])
        y1 = eb("y1", [P, T, D])
        y = eb("y", [P, T, D])
        zhat = eb("zhat", [P, T, D])
        zT_h = eb("zT_h", [P, S], F32R)
        zT_l = eb("zT_l", [P, S], F32R)
        reluT = eb("reluT", [P, FC, S])
        resid = [eb(f"resid{k}", [P, S]) for k in range(2)]
        y2 = [eb(f"y2{k}", [P, T, D]) for k in range(2)]
        x2s = [eb(f"x2s{k}", [P, T, D]) for k in range(2)]

        rw1 = eb("rw1", [P, HID])
        rw2 = eb("rw2", [P, E])
        x2T = eb("x2T", [P, S])
        z = eb("z", [P, S])
        enz = eb("enz", [P, S])
        enz1 = eb("enz1", [P, S])
        sigm = eb("sigm", [P, S])
        silu = eb("silu", [P, S])
        early.close()

        inputs = ctx.enter_context(ExitStack())
        hot = [sb(f"hot{k}", [P, T, SLOTS], F32R, inputs) for k in range(2)]
        xg = sb("xg", [P, E, 2, B, CAP], F32R, inputs)
        inputs.close()
        y_all = sb("y_all", [P, CH, B // EQ, EQ, NP, D], BF16)
        xg_end = sb("xg_end", [P, 2 * T * SLOTS + 2 * E * B * CAP - B * CH * NP * D // 2])
        wh = [sb(f"wh{k}", [P, 2, EF], F32R) for k in range(2)]
        wl = [sb(f"wl{k}", [P, 2, EF], F32R) for k in range(2)]
        tokens = [sb(f"tokens{k}", [P, SLOTS], BF16) for k in range(2)]
        x2h = [sb(f"x2h{k}", [P, T, D], F32R) for k in range(2)]
        x2l = [sb(f"x2l{k}", [P, T, D], F32R) for k in range(2)]
        sg = sb("sg", [P, EC, ES])
        hm = [sb(f"hm{k}", [P, EC, ES]) for k in range(2)]
        ys = [sb(f"ys{k}", [P, B // EQ, D]) for k in range(2)]
        rest = [sb(f"rest{k}", [P, B // EQ, D]) for k in range(2)]
        parts = [sb(f"parts{j}", [P, B // EQ, NP, D], BF16) for j in range(EQ)]
        onehot = sb("onehot", [P, B, CH, S], BF16)
        y3 = [sb(f"y3{j}", [P, T, D]) for j in range(4)]
        shift = [sb(f"shift{j}", [P, T]) for j in range(4)]
        outs = [sb(f"outs{j}", [P, T, D]) for j in range(4)]

        s_ld_feat = sem("s_ld_feat"); s_ld_vo = sem("s_ld_vo")
        s_ld_f1 = sem("s_ld_f1"); s_ld_f2 = sem("s_ld_f2")
        s_ld_r = sem("s_ld_r")
        s_xs = [sem(f"s_xs{k}") for k in range(2)]
        s_x_all = sem("s_x_all")
        s_const = sem("s_const")
        s_sel = sem("s_sel")
        s_prep_pe = sem("s_prep_pe"); s_prep_ev = sem("s_prep_ev")
        s_vo_pe = sem("s_vo_pe"); s_vo_ev = sem("s_vo_ev"); s_vo_h = sem("s_vo_h")
        s_f1_pe = sem("s_f1_pe"); s_f1_ev = sem("s_f1_ev")
        s_xt = sem("s_xt"); s_xTh = sem("s_xTh"); s_xTl = sem("s_xTl")
        s_proj0 = sem("s_proj0"); s_proj1 = sem("s_proj1")
        s_negmax = sem("s_negmax"); s_exp0 = sem("s_exp0"); s_exp = sem("s_exp")
        s_v = sem("s_v"); s_vs = sem("s_vs")
        s_ft0 = sem("s_ft0"); s_ft1 = sem("s_ft1"); s_feat = sem("s_feat")
        s_sc = sem("s_sc"); s_diag = sem("s_diag"); s_cross = sem("s_cross")
        s_av = sem("s_av"); s_den = sem("s_den"); s_rden = sem("s_rden"); s_y1 = sem("s_y1")
        s_y = sem("s_y"); s_st = sem("s_st"); s_mv = sem("s_mv")
        s_ve = sem("s_ve"); s_rstd = sem("s_rstd"); s_zhat = sem("s_zhat")
        s_zt = sem("s_zt"); s_zTh = sem("s_zTh"); s_zTl = sem("s_zTl")
        s_f1a = sem("s_f1a"); s_f1b = sem("s_f1b"); s_relu = sem("s_relu")
        s_f2 = sem("s_f2"); s_resid = sem("s_resid"); s_y2 = sem("s_y2")
        s_st2 = sem("s_st2"); s_mv2 = sem("s_mv2"); s_ve2 = sem("s_ve2"); s_rstd2 = sem("s_rstd2")
        s_x2 = sem("s_x2"); s_x2cp = sem("s_x2cp"); s_x2t = sem("s_x2t"); s_x2T = sem("s_x2T")
        s_hid = sem("s_hid"); s_z = sem("s_z"); s_enz = sem("s_enz"); s_enz1 = sem("s_enz1"); s_sigm = sem("s_sigm")
        s_silu = sem("s_silu"); s_lgp = sem("s_lgp"); s_lgs = sem("s_lgs")
        s_lst = [sem(f"s_lst{k}") for k in range(2)]
       
        s_top = [sem(f"s_top{g}") for g in range(G)]
        s_texp = sem("s_texp"); s_lists = sem("s_lists"); s_tpe = sem("s_tpe"); s_maps = sem("s_maps")
        s_bc = sem("s_bc"); s_tokens = sem("s_tokens"); s_hot = sem("s_hot"); s_x2h = sem("s_x2h"); s_x2l = sem("s_x2l")
        s_g = sem("s_g"); s_xgh = sem("s_xgh"); s_xgl = sem("s_xgl")
        s_ewgv = [sem(f"s_ewgv{m}") for m in range(2)]; s_ewdn = [sem(f"s_ewdn{m}") for m in range(2)]
        s_wh = sem("s_wh"); s_wl = sem("s_wl")
        s_gv0 = sem("s_gv0"); s_gv1 = sem("s_gv1"); s_sg0 = sem("s_sg0"); s_sg1 = sem("s_sg1")
        s_h0 = sem("s_h0"); s_h1a = sem("s_h1a"); s_h1 = sem("s_h1"); s_yp = sem("s_yp"); s_ys = sem("s_ys")
        s_b1 = sem("s_b1"); s_r1 = sem("s_r1"); s_b2 = sem("s_b2"); s_b3 = sem("s_b3")
        s_perm = [sem(f"s_perm{j}") for j in range(EQ)]
        s_onehot = sem("s_onehot"); s_c = sem("s_c"); s_y3 = sem("s_y3"); s_st3 = sem("s_st3")
        s_mv3 = sem("s_mv3"); s_ve3 = sem("s_ve3"); s_rstd3 = sem("s_rstd3"); s_fin = sem("s_fin")
        s_shift = sem("s_shift")
        s_out = [sem(f"s_out{j}") for j in range(4)]

        def after(eng, s, n):
            if isinstance(n, int) and n < 0:
                return
            eng.wait_ge(s, n + 1)

        def live(n, count):
            return not isinstance(n, int) or 0 <= n < count

        def pipeline(eng, body, count, before, behind, turn=2, lo=4):
            hi = (count - before) // turn * turn
            for i in range(-before, lo):
                body(i, i // turn, i % turn)
            with eng.Fori(lo // turn, hi // turn) as h:
                for k in range(turn):
                    body(h * turn + k, h, k)
            for i in range(hi, count + behind):
                body(i, i // turn, i % turn)

        AHEAD = 2

        def one_hot(eng, k):
            for t in range(T):
                op = eng.tensor_scalar(hot[k][:, t, :], tokens[k][:], tok[:, t:t + 1], None, ALU.is_equal)
            op.then_inc(s_hot, 1)

        block = ctx.enter_context(nc.Block())

        @block.sync
        def _(sp):

            def fixed(n):
                return n if isinstance(n, int) else sp.snap(n)

            sp.dma_start(om_raw[:], omega.unsqueeze(1).to_broadcast([M, H, DH])).then_inc(s_ld_feat, 16)
            sp.dma_start(w_raw[:, 1, :], Wk).then_inc(s_ld_feat, 16)
            sp.dma_start(wo[:], Wo).then_inc(s_ld_vo, 16)
            sp.dma_start(xs[1][:], x[1].rearrange("(t p) d -> p t d", p=P)).then_inc(s_xs[1], 16)
            sp.dma_start(wf1[:], W1).then_inc(s_ld_f1, 16)
            with nc.allow_non_contiguous_dma(reason="bias and scale vectors as columns"):
                sp.dma_start(b1c[:], b1.rearrange("(c p) -> p c", p=P)).then_inc(s_ld_f1, 16)
                sp.dma_start(gam[:], gamma.rearrange("(p a) -> p a", a=1)).then_inc(s_ld_f1, 16)
                sp.dma_start(bet[:], beta.rearrange("(p a) -> p a", a=1)).then_inc(s_ld_f1, 16)
            for t in range(T):
                sp.dma_start(x_all[:, :, t * D:(t + 1) * D],
                             x[:, t * P:(t + 1) * P, :].rearrange("b p d -> p b d")).then_inc(s_x_all, 16)
            sp.dma_start(wf2[:], W2.rearrange("(c p) d -> p c d", p=P)).then_inc(s_ld_f2, 16)
            for t in range(T):
                sp.dma_start(b2r[:, t, :], b2.rearrange("(a d) -> a d", a=1).to_broadcast([P, D])).then_inc(s_ld_f2, 16)
            sp.dma_start(rw1[:], router_w1).then_inc(s_ld_r, 16)
            sp.dma_start(rw2[:], router_w2).then_inc(s_ld_r, 16)

            def load_gate_value(e, m):
                e = ds(fixed(e), 2)
                for n, w in enumerate((w1, w2)):
                    sp.dma_start(wgv[m][:, :, n, :], w[e].rearrange("e d f -> d e f")).then_inc(s_ewgv[m], 16)

            def load_down(e, m):
                sp.dma_start(wdn[m][:].rearrange("p e c d -> p (e c) d"),
                             w3[ds(fixed(e), 2)].rearrange("e (c p) d -> p (e c) d", p=P)).then_inc(s_ewdn[m], 16)

            def loads(i, k):
                after(sp, s_xt, i - 2)
                sp.dma_start(xs[k][:], x[ds(i, 1)].rearrange("b (t p) d -> p (b t) d", p=P)).then_inc(s_xs[k], 16)

            def rows(b):
                after(sp, s_lgs, b)
                row = b % BG * E
                sp.dma_start(lg[row:row + E, b // BG, :], lgs[b % 2][:]).then_inc(s_lst[b % 2], 16)

            for i in range(2, B):
                loads(i, i % 2)
                if i >= 8:
                    rows(i - 8)
            for m in range(2):
                load_gate_value(2 * m, m)
                load_down(2 * m, m)
            for b in range(B - 8, B):
                rows(b)

            def regroup(c, j):
                chunk, done = ds(fixed(c + 0), 1), fixed(c * EQ + (j + 1))
                sp.wait_ge(s_b3, done)
                for r in range(EQ):
                    sp.dma_start(y_all[CAP * j:CAP * (j + 1), chunk, :, r, :, :].rearrange("p c q n d -> p (c q) (n d)"),
                                 parts[j][CAP * r:CAP * (r + 1), :, :, :].rearrange("p q n d -> p q (n d)")).then_inc(s_perm[j], 16)

            def reload(c, m):
                def free(s, e, load, m):
                    if isinstance(e, int) and e + EQ >= E:
                        return
                    done = fixed(e + 2)
                    sp.wait_ge(s, done)
                    load(e + EQ, m)

                free(s_wl, c * EQ + (2 * m + 2), load_gate_value, 1 - m)
                free(s_yp, c * EQ + 2 * m, load_down, m)

            def turn(c):
                for j in range(EQ):
                    if j % 2 == 0:
                        reload(c, j // 2)
                    regroup(c, j)

            sp.wait_ge(s_wl, 2)
            load_gate_value(EQ, 0)
            with sp.Fori(0, CH - 2) as c:
                turn(c)
            for c in range(CH - 2, CH):
                turn(c)

            with sp.Fori(0, B // 4) as h:
                for j in range(4):
                    b, done = sp.snap(h * 4 + j), sp.snap(h * 4 + (j + 1))
                    sp.wait_ge(s_fin, done)
                    sp.dma_start(out[ds(b, 1)].rearrange("b (t p) d -> p (b t) d", p=P), outs[j][:]).then_inc(s_out[j], 16)
            for j in range(4):
                sp.wait_ge(s_out[j], 16 * (B // 4))

        @block.gpsimd
        def _(pool):
            pool.memset(ident[:], 0.0).then_inc(s_const, 1)
            pool.memset(mask[:], 1.0).then_inc(s_const, 1)
            pool.memset(minus_half[:], -0.5).then_inc(s_const, 1)
            pool.memset(inner_eps[:], INNER_EPS).then_inc(s_const, 1)
            pool.memset(ln_eps[:], LN_EPS).then_inc(s_const, 1)
            for k in range(2):
                pool.memset(vs[k][:, :, :, D:D + 1], 1.0).then_inc(s_const, 1)
            pool.iota(iota_i[:], pattern=[[1, S]], base=0, channel_multiplier=0).then_inc(s_const, 1)
            pool.iota(tok_i[:], pattern=[[P, T]], base=0, channel_multiplier=1).then_inc(s_const, 1)
            pool.wait_ge(s_const, 9)
            pool.affine_select(out=ident[:], in_=ident[:], compare_op=ALU.not_equal, fill=1.0,
                               base=0, pattern=[[-1, P]], channel_multiplier=1).then_inc(s_const, 1)
            pool.affine_select(out=mask[:], in_=mask[:], compare_op=ALU.is_ge, fill=0.0,
                               base=0, pattern=[[0, T * H], [1, P]], channel_multiplier=-1).then_inc(s_const, 1)

            def inv_std(i, s_var, s_eps, s_done, q, eps):
                after(pool, s_var, i)
                pool.tensor_tensor(ve[q][:], mv[q][:, :, 1], eps[:], ALU.add).then_inc(s_eps, 1)
                after(pool, s_eps, i)
                pool.tensor_tensor(rstd[q][:], ve[q][:], minus_half[:], ALU.pow).then_inc(s_done, 1)

            def layer(i, h, k):
                if live(i, B):
                    if isinstance(i, int) and i == 0:
                        pool.wait_ge(s_ld_f2, 16 * (1 + T))
                        pool.wait_ge(s_x_all, 16 * T)
                    after(pool, s_y2, i - 2)
                    pool.tensor_tensor(resid[k][:].unsqueeze(1), x_all[:, ds(i, 1), :],
                                       b2r[:].rearrange("p t d -> p (t d)").unsqueeze(1), ALU.add).then_inc(s_resid, 1)
                if live(i - 2, B):
                    n = i - 2
                    after(pool, s_x2, n)
                    pool.tensor_copy(x2_all[:, ds(n, 1), :],
                                     x2s[k][:].rearrange("p t d -> p (t d)").unsqueeze(1)).then_inc(s_x2cp, 1)
                if live(i, B):
                    after(pool, s_zhat, i - 1)
                    inv_std(i, s_mv, s_ve, s_rstd, 2, inner_eps)
                if live(i - 1, B):
                    after(pool, s_x2, i - 3)
                    inv_std(i - 1, s_mv2, s_ve2, s_rstd2, 1 - k, ln_eps)

            pipeline(pool, layer, B, 2, 2)

            def gather(i, h, j):
                k = j % 2
                if isinstance(i, int) and 0 <= i < AHEAD:
                    after(pool, s_tokens, i)
                    one_hot(pool, k)
                if live(i + 1, B):
                    after(pool, s_x2h, i + 1)
                    after(pool, s_g, i - 1)
                    pool.tensor_tensor(x2l[1 - k][:].rearrange("p t d -> p (t d)").unsqueeze(1), x2_all[:, ds(i + 1, 1), :],
                                       x2h[1 - k][:].bitcast(F32).rearrange("p t d -> p (t d)").unsqueeze(1),
                                       ALU.subtract).then_inc(s_x2l, 1)

            pipeline(pool, gather, B, 1, 0, 4)

            def expert(e, h, j):
                k = j % 2
                if live(e, E):
                    after(pool, s_wh, e)
                    after(pool, s_gv1, e - 2)
                    pool.tensor_tensor(wl[k][:], wgv[j // 2][:, j % 2], wh[k][:].bitcast(F32), ALU.subtract).then_inc(s_wl, 1)

            pipeline(pool, expert, E, 0, 0, EQ)

            def scatter(i, h, j):
                if live(i, B):
                    after(pool, s_fin, i - 4)
                    inv_std(i, s_mv3, s_ve3, s_rstd3, j, ln_eps)

            pipeline(pool, scatter, B, 0, 0, 4)

        @block.scalar
        def _(act):
            act.dma_start(w_raw[:, 0, :], Wq).then_inc(s_ld_feat, 16)
            act.dma_start(w_raw[:, 2, :], Wv).then_inc(s_ld_vo, 16)
            act.dma_start(xs[0][:], x[0].rearrange("(t p) d -> p t d", p=P)).then_inc(s_xs[0], 16)

            def high_part(j, k):
                act.activation(wh[k][:], wgv[j // 2][:, j % 2], ACT.Copy).then_inc(s_wh, 1)

            def exps(t):
                for f in range(NF):
                    n = t * NF + f
                    op = act.activation(feat[:, n, :], ps(t)[:, f * M:(f + 1) * M], ACT.Exp, bias=negmax[:, n:n + 1])
                op.then_inc((s_exp0, s_exp)[t], 1)

            def layer(i, h, k):
                if live(i, B):
                    after(act, s_ft0, i)
                    act.activation(featT[:, 0:H, :].rearrange("p f s -> p (f s)"), ps(2), ACT.Copy, bias=FEAT_EPS, scale=FEAT_SCALE)
                    after(act, s_ft1, i)
                    act.activation(featT[:, H:, :].rearrange("p f s -> p (f s)"), ps(3), ACT.Copy, bias=FEAT_EPS,
                                   scale=FEAT_SCALE).then_inc(s_feat, 1)
                if live(i - 3, B):
                    after(act, s_x2t, i - 3)
                    act.activation(x2T[:], ps(5)[:, 0:S], ACT.Copy).then_inc(s_x2T, 1)
                if live(i - 1, B):
                    after(act, s_zt, i - 1)
                    act.activation(zT_h[:], ps(7)[:, 0:S], ACT.Copy).then_inc(s_zTh, 1)
                if live(i + 1, B):
                    after(act, s_v, i + 1)
                    act.activation(vs[1 - k][:, :, :, 0:D], ps(6).rearrange("p (t h d) -> p t h d", t=T, h=H),
                                   ACT.Copy).then_inc(s_vs, 1)
                if live(i, B):
                    after(act, s_sc, i)
                    act.activation(cross[:].rearrange("p h s -> p (h s)"), ps(5)[:, 0:H * P], ACT.Copy).then_inc(s_cross, 1)
                if live(i - 1, B):
                    if isinstance(i, int) and i == 1:
                        act.wait_ge(s_f1_ev, 3)
                    for c in range(FC):
                        if c % 2 == 0:
                            after(act, (s_f1a, s_f1b)[c // 2], i - 1)
                        op = act.activation(reluT[:, c, :], ps(2 + c // 2)[:, c % 2 * S:(c % 2 + 1) * S], ACT.Relu,
                                            bias=b1s[:, c:c + 1])
                    op.then_inc(s_relu, 1)
                if live(i - 3, B):
                    after(act, s_hid, i - 3)
                    after(act, s_silu, i - 4)
                    act.activation(enz[:], ps(6)[:, 0:S], ACT.Exp, scale=-1.0).then_inc(s_enz, 1)
                    act.activation(z[:], ps(6)[:, 0:S], ACT.Copy).then_inc(s_z, 1)
                if live(i + 1, B):
                    after(act, s_negmax, i + 1)
                    for t in range(T):
                        exps(t)
                if live(i + 2, B):
                    after(act, s_xt, i + 2)
                    act.activation(xT_h[:], ps(0)[:, 0:S], ACT.Copy).then_inc(s_xTh, 1)
                if live(i - 4, B):
                    after(act, s_lgp, i - 4)
                    if not isinstance(i, int) or i >= 6:
                        act.wait_ge(s_lst[k], h * 16 - 32)
                    act.activation(lgs[k][:], ps(6)[0:E, 0:S], ACT.Copy).then_inc(s_lgs, 1)
                if isinstance(i, int) and i == B - 1:
                    row_exps(0)

            def row_exps(g):
                act.wait_ge(s_top[g], 1)
                act.activation(lg[:, g, :], lg[:, g, :], ACT.Exp, bias=nmx[:, g:g + 1],
                               accum_out=ssum[:, g:g + 1]).then_inc(s_texp, 1)

            layer(-2, -1, 0)
            act.wait_ge(s_vo_pe, 2)
            for h in range(H):
                act.activation(wvo_h[:, h * D:(h + 1) * D], ps(4 + h)[:, 0:D], ACT.Copy).then_inc(s_vo_h, 1)
            pipeline(act, layer, B, 1, 4, lo=6)

            def gather(i, h, j):
                k = j % 2
                if live(i + 1, B):
                    after(act, s_bc, i + 1)
                    after(act, s_hot, i - 1)
                    act.activation(tokens[1 - k][:], ps(1 - k), ACT.Copy).then_inc(s_tokens, 1)
                if live(i - 1, B):
                    after(act, s_g, i - 1)
                    act.activation(xg[:, :, 0, ds(i - 1, 1), :].rearrange("p e b c -> p (e b) c"),
                                   ps(2 + (j - 1) % 4).rearrange("p (e c) -> p e c", e=E), ACT.Copy).then_inc(s_xgh, 1)
                if live(i + 1, B):
                    after(act, s_g, i - 1)
                    act.activation(x2h[1 - k][:].rearrange("p t d -> p (t d)").unsqueeze(1), x2_all[:, ds(i + 1, 1), :],
                                   ACT.Copy).then_inc(s_x2h, 1)
                if isinstance(i, int) and i == 0:
                    row_exps(1)
                    for e in range(2):
                        act.wait_ge(s_ewgv[0], 32)
                        high_part(e, e)

            act.wait_ge(s_x2cp, B)
            pipeline(act, gather, B, 1, 1, 4)

            def expert(e, h, j):
                k = j % 2
                if live(e - 1, E):
                    after(act, s_gv0, e - 1)
                    after(act, s_h0, e - 2)
                    act.activation(sg[:, 0, :], ps(0), ACT.Silu).then_inc(s_sg0, 1)
                if live(e - 3, E):
                    after(act, s_ys, e - 3)
                    at = (j - 3) % EQ
                    if not isinstance(e, int) or e >= EQ + 3:
                        act.wait_ge(s_perm[at], h * (16 * EQ) - (16 * EQ if j < 3 else 0))
                    act.activation(parts[at][:, :, 0, :], ys[1 - k][:], ACT.Copy).then_inc(s_b1, 1)
                if live(e - 1, E):
                    after(act, s_gv1, e - 1)
                    after(act, s_h1, e - 2)
                    act.activation(sg[:, 1, :], ps(2), ACT.Silu).then_inc(s_sg1, 1)
                if live(e - 2, E):
                    if isinstance(e, int) and e == 2:
                        act.wait_ge(s_maps, 2)
                    after(act, s_yp, e - 2)
                    after(act, s_r1, e - 4)
                    for q in range(B // EQ):
                        op = act.activation(ys[k][:, q, :], ps(4 + k)[:, q * D:(q + 1) * D], ACT.Copy,
                                            scale=slot_w[:, q, ds(e - 2, 1)])
                    op.then_inc(s_ys, 1)
                if live(e + 1, E) and not (isinstance(e, int) and e + 1 < 2):
                    turn = h + (j + 1) // EQ
                    act.wait_ge(s_ewgv[(j + 1) % EQ // 2], turn * 32 + 32)
                    after(act, s_gv1, e - 1)
                    high_part((j + 1) % EQ, 1 - k)
                if live(e - 3, E):
                    after(act, s_r1, e - 3)
                    act.activation(parts[(j - 3) % EQ][:, :, 1, :], rest[1 - k][:], ACT.Copy).then_inc(s_b2, 1)

            act.activation(silu_in[:], ln_eps[:], ACT.Silu)
            pipeline(act, expert, E, 1, 3, EQ, lo=2 * EQ)

            def scatter(i, h, j):
                if live(i, B):
                    after(act, s_shift, i)
                    if not isinstance(i, int) or i >= 4:
                        act.wait_ge(s_out[j], h * 16)
                    for t in range(T):
                        op = act.activation(outs[j][:, t, :], y3[j][:, t, :], ACT.Identity, bias=shift[j][:, t:t + 1],
                                            scale=rstd[j][:, t:t + 1])
                    op.then_inc(s_fin, 1)

            pipeline(act, scatter, B, 0, 0, 4)

        @block.vector
        def _(dve):
            dve.wait_ge(s_prep_pe, 1)
            dve.tensor_copy(wT[:, 0:2].rearrange("p n d -> p (n d)"), ps(7)[:, 0:2 * D]).then_inc(s_prep_ev, 1)
            dve.tensor_copy(omT[:], ps(7)[:, 2 * D:2 * D + M]).then_inc(s_prep_ev, 1)
            dve.wait_ge(s_vo_pe, 1)
            dve.tensor_copy(wT[:, 2], ps(3)[:, 0:D]).then_inc(s_vo_ev, 1)
            dve.wait_ge(s_prep_pe, 2)

            def split(n, h, w_part):
                return w_part[:].rearrange("p (n h m) -> p n h m", n=n, h=H)[:, :, h, :]

            for h in range(H):
                dve.tensor_scalar(split(2, h, wfeat_h), ps(1 + h)[:, 0:2 * M].rearrange("p (n m) -> p n m", n=2), SCALE, None,
                                  ALU.mult).then_inc(s_prep_ev, 1)
            dve.wait_ge(s_prep_ev, 2 + H)
            for h in range(H):
                dve.scalar_tensor_tensor(split(2, h, wfeat_l), ps(1 + h)[:, 0:2 * M].rearrange("p (n m) -> p n m", n=2), SCALE,
                                         split(2, h, wfeat_h).bitcast(F32), ALU.mult, ALU.subtract).then_inc(s_prep_ev, 1)

            dve.wait_ge(s_vo_h, H)
            for h in range(H):
                dve.tensor_tensor(wvo_l[:, h * D:(h + 1) * D], ps(4 + h)[:, 0:D], wvo_h[:, h * D:(h + 1) * D].bitcast(F32),
                                  ALU.subtract).then_inc(s_vo_ev, 1)

            def selectors():
                dve.wait_ge(s_const, 11)
                dve.tensor_reduce(m4[:], ident[:].rearrange("p (q j) -> p j q", j=EQ), AX.X, ALU.add).then_inc(s_sel, 1)
                dve.tensor_reduce(r32[:], ident[:].rearrange("p (q j) -> p q j", j=EQ), AX.X, ALU.add).then_inc(s_sel, 1)
                dve.tensor_reduce(m16[:], ident[:].rearrange("p (b e) -> p e b", e=E), AX.X, ALU.add).then_inc(s_sel, 1)
                dve.tensor_reduce(b8[:], ident[:].rearrange("p (b e) -> p b e", e=E), AX.X, ALU.add).then_inc(s_sel, 1)
                dve.tensor_copy(iota[:], iota_i[:]).then_inc(s_sel, 1)
                dve.tensor_copy(tok[:], tok_i[:]).then_inc(s_sel, 1)
                dve.tensor_reduce(re[:].rearrange("p (q e) -> p q e", e=E), ident[:].rearrange("p (q r e) -> p q e r", r=EQ, e=E),
                                  AX.X, ALU.add).then_inc(s_sel, 1)
                dve.wait_ge(s_sel, 7)
                dve.tensor_reduce(q4[:], b8[:].rearrange("p (q r) -> p r q", r=EQ), AX.X, ALU.add).then_inc(s_sel, 1)
                for g in range(G):
                    dve.tensor_copy(lb[:, g * BG:(g + 1) * BG, :], b8[:].unsqueeze(2).to_broadcast([P, BG, P])).then_inc(s_sel, 1)

            def ffn_weights():
                dve.wait_ge(s_ld_f1, 16 * 4)
                dve.tensor_scalar(wf1_h[:], wf1[:], gam[:], None, ALU.mult).then_inc(s_f1_ev, 1)
                dve.wait_ge(s_f1_ev, 1)
                dve.scalar_tensor_tensor(wf1_l[:], wf1[:], gam[:], wf1_h[:].bitcast(F32), ALU.mult, ALU.subtract)\
                   .then_inc(s_f1_ev, 1)
                dve.wait_ge(s_f1_pe, 1)
                dve.tensor_tensor(b1s[:], ps(7)[:, 0:FC], b1c[:], ALU.add).then_inc(s_f1_ev, 1)

            def sums(src, q, s_stats):
                for t in range(T):
                    op = dve.bn_stats(stats[q][:, t, :], src[:, t, :])
                op.then_inc(s_stats, 1)

            def moments(sums_at, q, s_done):
                for t in range(T):
                    op = dve.bn_aggr(mv[q][:, t, :], stats[sums_at][:, t, :])
                op.then_inc(s_done, 1)

            def normalise(dst, src, q, s_done):
                for t in range(T):
                    op = dve.tensor_scalar(dst[:, t, :], src[:, t, :], mv[q][:, t, 0:1], rstd[q][:, t:t + 1],
                                           ALU.subtract, ALU.mult)
                op.then_inc(s_done, 1)

            def divisor(n):
                after(dve, s_enz, n)
                dve.tensor_scalar(enz1[:], enz[:], EXP_MAX, 1.0, ALU.min, ALU.add).then_inc(s_enz1, 1)
                after(dve, s_enz1, n)
                dve.reciprocal(sigm[:, 0:P], enz1[:, 0:P])

            def divisor_rest(n):
                dve.reciprocal(sigm[:, P:S], enz1[:, P:S]).then_inc(s_sigm, 1)

            def hidden_product(n):
                after(dve, s_sigm, n)
                after(dve, s_z, n)
                after(dve, s_lgp, n - 1)
                dve.tensor_tensor(silu[:], z[:], sigm[:], ALU.mult).then_inc(s_silu, 1)

            def hidden_silu(n):
                divisor(n)
                divisor_rest(n)
                hidden_product(n)

            def low_zT(n):
                after(dve, s_zTh, n)
                dve.tensor_tensor(zT_l[:], ps(7)[:, 0:S], zT_h[:].bitcast(F32), ALU.subtract).then_inc(s_zTl, 1)

            def output(n, k):
                after(dve, s_rstd2, n)
                after(dve, s_x2t, n - 2)
                after(dve, s_x2cp, n - 2)
                normalise(x2s[k], y2[k], k, s_x2)

            def layer(i, h, k):
                if live(i - 4, B) and live(i, B):
                    divisor(i - 4)
                if live(i - 1, B):
                    low_zT(i - 1)
                if live(i - 4, B) and live(i, B):
                    divisor_rest(i - 4)
                if isinstance(i, int) and i >= B:
                    if live(i - 2, B):
                        output(i - 2, k)
                    if i == B:
                        hidden_silu(i - 4)
                    if live(i - 3, B):
                        hidden_silu(i - 3)
                    if i == B:
                        row_softmax(0)
                        top_tokens(0, 0)
                if live(i, B):
                    after(dve, s_sc, i)
                    dve.tensor_tensor(diag[:].rearrange("p n s -> p (n s)"), ps(4), mask[:].rearrange("p n s -> p (n s)"),
                                      ALU.mult).then_inc(s_diag, 1)
                    if live(i - 4, B):
                        hidden_product(i - 4)
                if live(i + 1, B):
                    after(dve, s_proj0, i + 1)
                    dve.tensor_reduce(negmax[:, 0:NF], ps(0).rearrange("p (f m) -> p f m", f=NF), AX.X, ALU.max,
                                      negate=True)
                    after(dve, s_proj1, i + 1)
                    dve.tensor_reduce(negmax[:, NF:], ps(1).rearrange("p (f m) -> p f m", f=NF), AX.X, ALU.max,
                                      negate=True).then_inc(s_negmax, 1)
                if live(i, B) and live(i - 2, B):
                    output(i - 2, k)
                if live(i, B):
                    after(dve, s_av, i)
                    av = bank[2][:, :, 0:H * (D + 1)].rearrange("p t (h d) -> p t h d", h=H)
                    dve.tensor_scalar(den[:].unsqueeze(3), av[:, :, :, D:D + 1], FEAT_EPS, None, ALU.add).then_inc(s_den, 1)
                    after(dve, s_den, i)
                    dve.reciprocal(rden[:], den[:]).then_inc(s_rden, 1)
                    after(dve, s_rden, i)
                    if isinstance(i, int) and i == 0:
                        dve.wait_ge(s_x_all, 16 * T)
                    for t in range(T):
                        op = dve.scalar_tensor_tensor(y1[:, t:t + 1, :], av[:, t:t + 1, 0, 0:D], rden[:, t, 0:1],
                                                      x_all[:, ds(i, 1), t * D:(t + 1) * D], ALU.mult, ALU.add)
                    op.then_inc(s_y1, 1)
                    after(dve, s_y1, i)
                    for t in range(T):
                        op = dve.scalar_tensor_tensor(y[:, t, :], av[:, t, 1, 0:D], rden[:, t, 1:2], y1[:, t, :],
                                                      ALU.mult, ALU.add)
                    op.then_inc(s_y, 1)
                    after(dve, s_y, i)
                    sums(y, 1, s_st)
                if isinstance(i, int) and i == -1:
                    selectors()
                if live(i + 2, B):
                    after(dve, s_xTh, i + 2)
                    if live(i, B):
                        after(dve, s_st, i)
                    dve.tensor_tensor(xT_l[:], ps(0)[:, 0:S], xT_h[:].bitcast(F32), ALU.subtract).then_inc(s_xTl, 1)
                elif live(i, B):
                    dve.wait_ge(s_st, i + 1)
                if live(i, B):
                    moments(1, 2, s_mv)
                if live(i - 1, B):
                    after(dve, s_f2, i - 1)
                    after(dve, s_resid, i - 1)
                    dve.tensor_tensor(y2[1 - k][:].rearrange("p t d -> p (t d)"), ps(7)[:, 0:S], resid[1 - k][:],
                                      ALU.add).then_inc(s_y2, 1)
                    after(dve, s_y2, i - 1)
                    sums(y2[1 - k], 0, s_st2)
                if live(i, B):
                    after(dve, s_rstd, i)
                    if live(i - 1, B):
                        after(dve, s_st2, i - 1)
                    normalise(zhat, y, 2, s_zhat)
                elif live(i - 1, B):
                    dve.wait_ge(s_st2, i)
                if live(i - 1, B):
                    moments(0, 1 - k, s_mv2)
                if isinstance(i, int) and i == -1:
                    ffn_weights()
                if isinstance(i, int) and i == B - 2:
                    row_maximum(0)
                if isinstance(i, int) and i == B:
                    top_tokens(0, 1)

            done = [0] * G

            def step(g, ins):
                done[g] += 1
                ins.then_inc(s_top[g], 1)
                dve.wait_ge(s_top[g], done[g])

            def row_maximum(g):
                for k in range(2):
                    dve.wait_ge(s_lst[k], 16 * (g + 1) * (BG // 2))
                step(g, dve.tensor_reduce(nmx[:, g:g + 1], lg[:, g, :], AX.X, ALU.max, negate=True))

            def row_softmax(g):
                dve.wait_ge(s_texp, g + 1)
                step(g, dve.reciprocal(rsum[:, g:g + 1], ssum[:, g:g + 1]))
                step(g, dve.tensor_scalar(lg[:, g, :], lg[:, g, :], rsum[:, g:g + 1], None, ALU.mult))

            def top_tokens(g, r):
                top = val[:, g, 8 * r:8 * r + 8]
                step(g, dve.max(top, lg[:, g, :]))
                step(g, dve.max_index(idx[:, g, 8 * r:8 * r + 8], top, lg[:, g, :]))
                if r < CAP // 8 - 1:
                    step(g, dve.match_replace(lg[:, g, :], top, lg[:, g, :], -1.0))

            def gather_list(g):
                step(g, dve.tensor_copy(idxf[:, g], idx[:, g]))
                dve.tensor_tensor(r3[:, g], idxf[:, g].unsqueeze(1).to_broadcast([P, E, CAP]),
                                  m16[:].unsqueeze(2).to_broadcast([P, E, CAP]), ALU.mult).then_inc(s_lists, 1)

            def slot_lists(g):
                step(g, dve.tensor_reduce(wsum[:, g:g + 1], val[:, g], AX.X, ALU.add))
                step(g, dve.tensor_scalar(wsum[:, g:g + 1], wsum[:, g:g + 1], WEIGHT_EPS, None, ALU.add))
                step(g, dve.reciprocal(wrec[:, g:g + 1], wsum[:, g:g + 1]))
                step(g, dve.tensor_scalar(wgt[:, g], val[:, g], wrec[:, g:g + 1], None, ALU.mult))
                dve.tensor_tensor(idx4[:, g], idxf[:, g].unsqueeze(1).to_broadcast([P, EQ, CAP]),
                                  m4[:].unsqueeze(2).to_broadcast([P, EQ, CAP]), ALU.mult)
                dve.tensor_tensor(wgt4[:, g], wgt[:, g].unsqueeze(1).to_broadcast([P, EQ, CAP]),
                                  q4[:].unsqueeze(2).to_broadcast([P, EQ, CAP]), ALU.mult).then_inc(s_tpe, 1)

            pipeline(dve, layer, B, 2, 3)
            for r in range(2, CAP // 8):
                top_tokens(0, r)
            gather_list(0)
            row_maximum(1)
            row_softmax(1)
            for r in range(CAP // 8):
                top_tokens(1, r)
            gather_list(1)
            slot_lists(0)

            def gather(i, h, j):
                k = j % 2
                if live(i, B) and not (isinstance(i, int) and i < AHEAD):
                    if isinstance(i, int) and i == AHEAD:
                        dve.wait_ge(s_hot, AHEAD)
                    after(dve, s_tokens, i)
                    after(dve, s_g, i - 2)
                    one_hot(dve, k)
                if live(i - 2, B):
                    after(dve, s_xgh, i - 2)
                    row = ds(i - 2, 1)
                    dve.tensor_tensor(xg[:, :, 1, row, :].rearrange("p e b c -> p (e b) c"),
                                      ps(2 + (j - 2) % 4).rearrange("p (e c) -> p e c", e=E),
                                      xg[:, :, 0, row, :].rearrange("p e b c -> p (e b) c").bitcast(F32),
                                      ALU.subtract).then_inc(s_xgl, 1)
            pipeline(dve, gather, B, 0, 2, 4)
            slot_lists(1)

            def expert(e, h, j):
                k = j % 2
                if live(e, E):
                    after(dve, s_yp, e - 2)
                    after(dve, s_sg0, e)
                    dve.tensor_tensor(hm[k][:, 0, :], sg[:, 0, :], ps(1), ALU.mult).then_inc(s_h0, 1)
                if live(e - 2, E):
                    after(dve, s_b1, e - 2)
                    after(dve, s_b3, e - 4)
                    dve.tensor_tensor(rest[k][:], ys[k][:], parts[(j - 2) % EQ][:, :, 0, :], ALU.subtract).then_inc(s_r1, 1)
                if live(e - 3, E):
                    at = (j - 3) % EQ
                    after(dve, s_b2, e - 3)
                    dve.tensor_tensor(parts[at][:, :, 2, :], rest[1 - k][:], parts[at][:, :, 1, :], ALU.subtract).then_inc(s_b3, 1)
                if live(e, E):
                    after(dve, s_sg1, e)
                    for cols, s in ((slice(0, ES // 2), s_h1a), (slice(ES // 2, ES), s_h1)):
                        dve.tensor_tensor(hm[k][:, 1, cols], sg[:, 1, cols], ps(3)[:, cols], ALU.mult).then_inc(s, 1)
                if isinstance(e, int) and e == 1:
                    dve.wait_ge(s_tpe, G + 1)
                    dve.tensor_copy(slot_tok[:], ps(6)[:, 0:B * CH]).then_inc(s_maps, 1)
                    dve.tensor_copy(slot_w[:].rearrange("p q e -> p (q e)"), ps(7)[:, 0:B // EQ * E]).then_inc(s_maps, 1)
                    dve.wait_ge(s_maps, 1)
                if live(e - 1, B):
                    for c in range(CH):
                        op = dve.tensor_scalar(onehot[:, ds(e - 1, 1), c, :], iota[:].unsqueeze(1),
                                               slot_tok[:, ds(e * CH + (c - CH), 1)], None, ALU.is_equal)
                    op.then_inc(s_onehot, 1)

            pipeline(dve, expert, E, 0, 3, EQ)

            def scatter(i, h, j):
                if live(i, B):
                    after(dve, s_c, i)
                    after(dve, s_fin, i - 4)
                    after(dve, s_st3, i - 1)
                    dve.tensor_tensor(y3[j][:], bank[j][:, :, 0:D], x2_all[:, ds(i, 1), :].rearrange("p a (t d) -> p (a t) d", t=T),
                                      ALU.add).then_inc(s_y3, 1)
                elif live(i - 1, B):
                    dve.wait_ge(s_st3, i)
                if live(i - 1, B):
                    moments((j - 1) % 2, (j - 1) % 4, s_mv3)
                if live(i, B):
                    after(dve, s_y3, i)
                    sums(y3[j], j % 2, s_st3)
                if live(i - 2, B):
                    at = (j - 2) % 4
                    after(dve, s_rstd3, i - 2)
                    dve.scalar_tensor_tensor(shift[at][:], mv[at][:, :, 0], -1.0, rstd[at][:], ALU.mult, ALU.mult).then_inc(s_shift, 1)

            pipeline(dve, scatter, B, 0, 2, 4)

        @block.tensor
        def _(pe):
            pe.wait_ge(s_const, 11)
            pe.wait_ge(s_ld_feat, 16 * 3)
            for n in range(2):
                pe.transpose(ps(7)[:, n * D:(n + 1) * D], w_raw[:, n, :], ident[:])
            pe.transpose(ps(7)[:, 2 * D:2 * D + M], om_raw[:].rearrange("p h d -> p (h d)"), ident[:]).then_inc(s_prep_pe, 1)
            pe.wait_ge(s_ld_vo, 16 * 2)
            pe.transpose(ps(3)[:, 0:D], w_raw[:, 2, :], ident[:]).then_inc(s_vo_pe, 1)
            def transposes(dst, src, s):
                for t in range(T):
                    op = pe.transpose(dst[:, t * P:(t + 1) * P], src[:, t, :], ident[:])
                op.then_inc(s, 1)

            pe.wait_ge(s_prep_ev, 2)
            for n in range(2):
                for h in range(H):
                    head = slice(h * DH, (h + 1) * DH)
                    op = pe.matmul(ps(1 + h)[:, n * M:(n + 1) * M], wT[head, n, :], omT[head, :], start=True, stop=True)
            op.then_inc(s_prep_pe, 1)
            pe.wait_ge(s_xs[0], 16)
            transposes(ps(0), xs[0], s_xt)
            pe.wait_ge(s_vo_ev, 1)
            for h in range(H):
                head = slice(h * DH, (h + 1) * DH)
                op = pe.matmul(ps(4 + h)[:, 0:D], wT[head, 2, :], wo[head, :], start=True, stop=True)
            op.then_inc(s_vo_pe, 1)

            def features(i):
                after(pe, s_exp, i)
                for f in range(NF):
                    for t in range(T):
                        op = pe.transpose(ps(2 + f // 2)[:, f % 2 * S + t * P:f % 2 * S + (t + 1) * P],
                                          feat[:, t * NF + f, :], ident[:])
                    if f % 2:
                        op.then_inc((s_ft0, s_ft1)[f // 2], 1)

            def project(i):
                first = isinstance(i, int) and i == 0
                if first:
                    pe.wait_ge(s_prep_ev, 2 + H)
                    pe.wait_ge(s_vo_h, H)
                after(pe, s_xTl, i)
                after(pe, s_exp, i - 1)
                after(pe, s_z, i - 5)
                after(pe, s_lgs, i - 6)
                for t in range(T):
                    tile = slice(t * P, (t + 1) * P)
                    for n, (part, wf, wvo) in enumerate(((xT_l, wfeat_h, wvo_h), (xT_h, wfeat_h, wvo_h), (xT_h, wfeat_l, wvo_l))):
                        flags = dict(start=(n == 0), stop=(n == 2))
                        if first and n == 2:
                            pe.wait_ge(s_prep_ev, 2 + 2 * H)
                            pe.wait_ge(s_vo_ev, 1 + H)
                        op = pe.matmul(ps(t), part[:, tile], wf[:], **flags)
                        if n == 2:
                            op.then_inc((s_proj0, s_proj1)[t], 1)
                        op = pe.matmul(ps(6)[:, t * H * D:(t + 1) * H * D], part[:, tile], wvo[:], **flags)
                op.then_inc(s_v, 1)

            def qk(i):
                after(pe, s_feat, i)
                after(pe, s_x2T, i - 3)
                after(pe, s_y, i - 1)
                for h in range(H):
                    q, kf = featT[:, h, :], featT[:, H + h, :]
                    for t in range(T):
                        tile = slice(t * P, (t + 1) * P)
                        pe.matmul(ps(4)[:, (h * T + t) * P:(h * T + t + 1) * P], kf[:, tile], q[:, tile], start=True, stop=True)
                    op = pe.matmul(ps(5)[:, h * P:(h + 1) * P], kf[:, 0:P], q[:, P:S], start=True, stop=True)
                op.then_inc(s_sc, 1)

            def attend(i, k):
                after(pe, s_diag, i)
                after(pe, s_cross, i)
                after(pe, s_vs, i)
                w = D + 1
                for h in range(H):
                    pe.matmul(ps(4)[:, h * w:(h + 1) * w], diag[:, h * T, :], vs[k][:, 0, h, :], start=True, stop=True)
                for h in range(H):
                    to = ps(5)[:, h * w:(h + 1) * w]
                    pe.matmul(to, cross[:, h, :], vs[k][:, 0, h, :], start=True, stop=False)
                    op = pe.matmul(to, diag[:, h * T + 1, :], vs[k][:, 1, h, :], start=False, stop=True)
                op.then_inc(s_av, 1)

            def ffn_up(i):
                if isinstance(i, int) and i == 0:
                    pe.wait_ge(s_f1_ev, 3)
                after(pe, s_zTl, i)
                for c in range(FC):
                    to, cols = ps(2 + c // 2)[:, c % 2 * S:(c % 2 + 1) * S], slice(c * P, (c + 1) * P)
                    pe.matmul(to, wf1_h[:, cols], zT_l[:], start=True, stop=False)
                    pe.matmul(to, wf1_h[:, cols], zT_h[:], start=False, stop=False)
                    op = pe.matmul(to, wf1_l[:, cols], zT_h[:], start=False, stop=True)
                    if c % 2:
                        op.then_inc((s_f1a, s_f1b)[c // 2], 1)

            def ffn_down(i, t):
                for c in range(FC):
                    op = pe.matmul(ps(7)[:, t * D:(t + 1) * D], reluT[:, c, t * P:(t + 1) * P], wf2[:, c, :],
                                   start=(c == 0), stop=(c == FC - 1))
                if t == T - 1:
                    op.then_inc(s_f2, 1)

            def layer(i, h, k):
                if live(i, B):
                    features(i)
                if live(i - 3, B):
                    after(pe, s_x2, i - 3)
                    if live(i - 1, B):
                        after(pe, s_y, i - 1)
                    transposes(ps(5), x2s[1 - k], s_x2t)
                if live(i + 1, B):
                    project(i + 1)
                if live(i - 1, B):
                    after(pe, s_zhat, i - 1)
                    after(pe, s_y2, i - 2)
                    transposes(ps(7), zhat, s_zt)
                if live(i, B):
                    qk(i)
                if live(i - 3, B):
                    if isinstance(i, int) and i == 3:
                        pe.wait_ge(s_ld_r, 16 * 2)
                    after(pe, s_x2T, i - 3)
                    if live(i + 1, B):
                        after(pe, s_vs, i + 1)
                    else:
                        after(pe, s_lgs, i - 5)
                    pe.matmul(ps(6)[:, 0:S], rw1[:], x2T[:], start=True, stop=True).then_inc(s_hid, 1)
                if live(i - 1, B):
                    ffn_up(i - 1)
                if live(i, B):
                    attend(i, k)
                if live(i - 1, B):
                    if isinstance(i, int) and i == 1:
                        pe.wait_ge(s_ld_f2, 16 * (1 + T))
                    after(pe, s_relu, i - 1)
                    ffn_down(i - 1, 0)
                    ffn_down(i - 1, 1)
                if live(i - 4, B):
                    after(pe, s_silu, i - 4)
                    if live(i - 3, B):
                        after(pe, s_z, i - 3)
                    else:
                        after(pe, s_lgs, i - 5)
                    pe.matmul(ps(6)[0:E, 0:S], rw2[:], silu[:], start=True, stop=True).then_inc(s_lgp, 1)
                if live(i + 2, B):
                    if isinstance(i, int):
                        pe.wait_ge(s_xs[k], 16 * (h + 2))
                    else:
                        pe.wait_ge(s_xs[k], h * 16 + 32)
                    if live(i + 1, B):
                        after(pe, s_exp0, i + 1)
                    transposes(ps(0), xs[k], s_xt)
                if isinstance(i, int) and i == -1:
                    pe.wait_ge(s_ld_f1, 16 * 4)
                    for c in range(FC):
                        op = pe.matmul(ps(7)[:, c:c + 1], wf1[:, c * P:(c + 1) * P], bet[:], start=True, stop=True)
                    op.then_inc(s_f1_pe, 1)

            pipeline(pe, layer, B, 1, 4, lo=6)

            pe.wait_ge(s_lists, 1)

            def gather(i, h, j):
                k = j % 2
                if live(i + 2, B):
                    n = i + 2
                    after(pe, s_tokens, i)
                    g = n // BG
                    pe.matmul(ps(k), lb[:, ds(n, 1), :].rearrange("p a m -> p (a m)"),
                              r3[:, ds(g, 1)].rearrange("p a e c -> p (a e c)"), start=True, stop=True).then_inc(s_bc, 1)
                if live(i, B):
                    after(pe, s_hot, i)
                    after(pe, s_x2l, i)
                    after(pe, s_xgl, i - 4)
                    for t in range(T):
                        for part in (x2l, x2h):
                            op = pe.matmul(ps(2 + j), part[k][:, t, :], hot[k][:, t, :],
                                           start=(t == 0 and part is x2l), stop=(t == T - 1 and part is x2h))
                    op.then_inc(s_g, 1)
                if isinstance(i, int) and i == AHEAD:
                    pe.wait_ge(s_lists, G)

            pipeline(pe, gather, B, 2, 0, 4)

            def expert(e, h, j):
                k = j % 2

                def gate_value(c, s):
                    xh, xl = (xg[:, ds(e, 1), n].rearrange("p a b c -> p (a b c)") for n in range(2))
                    for n in range(2):
                        wide = slice(c * P, (c + 1) * P)
                        to = ps(2 * c + n)
                        pe.matmul(to, wl[k][:, n, wide], xh, start=True, stop=False)
                        pe.matmul(to, wh[k][:, n, wide], xl, start=False, stop=False)
                        op = pe.matmul(to, wh[k][:, n, wide], xh, start=False, stop=True)
                    op.then_inc(s, 1)

                if live(e, E):
                    after(pe, s_wl, e)
                    after(pe, s_h0, e - 1)
                    gate_value(0, s_gv0)
                if live(e - 1, E):
                    after(pe, s_h1a, e - 1)
                    after(pe, s_ys, e - 3)
                    pe.wait_ge(s_ewdn[(j - 1) % EQ // 2], h * 16 + (16 if j else 0))
                    for q in range(B // EQ):
                        if q == B // EQ // 2:
                            after(pe, s_h1, e - 1)
                        for c in range(EC):
                            op = pe.matmul(ps(5 - k)[:, q * D:(q + 1) * D], hm[1 - k][:, c, q * P:(q + 1) * P],
                                           wdn[(j - 1) % EQ // 2][:, (j - 1) % 2, c, :], start=(c == 0), stop=(c == EC - 1))
                    op.then_inc(s_yp, 1)
                if live(e, E):
                    gate_value(1, s_gv1)
                if isinstance(e, int) and e == 1:
                    pe.wait_ge(s_tpe, G)
                    for g in range(G):
                        cols = slice(g * P // EQ, (g + 1) * P // EQ)
                        pe.matmul(ps(6)[:, cols], idx4[:, g].rearrange("p j c -> p (j c)"), r32[:], start=True, stop=True)
                        op = pe.matmul(ps(7)[:, cols], wgt4[:, g].rearrange("p j c -> p (j c)"), re[:], start=True, stop=True)
                    op.then_inc(s_tpe, 1)

            pe.wait_ge(s_xgl, B)
            pipeline(pe, expert, E, 0, 1, EQ)

            y_flat = y_all[:].rearrange("p c q r n d -> p c (q r) n d")

            def scatter(i, chunks):
                for t in range(T):
                    for c in chunks:
                        for n in reversed(range(NP)):
                            op = pe.matmul(bank[i % 4][:, t, 0:D], onehot[:, i, c, t * P:(t + 1) * P],
                                           y_flat[:, c, i, n, :],
                                           start=(c == 0 and n == NP - 1), stop=(c == CH - 1 and n == 0))
                if CH - 1 in chunks:
                    op.then_inc(s_c, 1)

            pe.wait_ge(s_onehot, B)
            pe.wait_ge(s_h1, E)
            pe.wait_ge(s_ys, E)
            for chunks in (range(CH - 1), range(CH - 1, CH)):
                for j in range(EQ):
                    pe.wait_ge(s_perm[j], 16 * EQ * chunks.stop)
                for i in range(4):
                    scatter(i, chunks)
            for i in range(4, B):
                after(pe, s_y3, i - 4)
                scatter(i, range(CH))


_INS = ['L0_attn_batch', 'L0_attn_Wq', 'L0_attn_Wk', 'L0_attn_Wv', 'L0_attn_Wo', 'L0_attn_omega', 'L0_attn_W1',
        'L0_attn_b1', 'L0_attn_W2', 'L0_attn_b2', 'L0_attn_gamma', 'L0_attn_beta', 'L0_ffn_router_w1',
        'L0_ffn_router_w2', 'L0_ffn_w1', 'L0_ffn_w2', 'L0_ffn_w3']


def kernel(**inputs):
    import numpy as _np
    import concourse.bacc as _bacc
    from concourse import mybir as _mybir
    from concourse.bass_utils import run_bass_kernel_spmd as _run

    nc = _bacc.Bacc("TRN2", target_bir_lowering=False, num_devices=1)
    arrays, args = {}, []
    for name in _INS:
        a = _np.ascontiguousarray(inputs[name])
        arrays[f"in_{name}_dram"] = a
        args.append(nc.dram_tensor(f"in_{name}_dram", a.shape, _mybir.dt.from_np(a.dtype), kind="ExternalInput").ap())
    shape = inputs['L0_attn_batch'].shape
    res = nc.dram_tensor("out_0_dram", shape, _mybir.dt.float32, kind="ExternalOutput").ap()
    post_ln_block(nc, *args, res)
    r = _run(nc, [arrays], core_ids=[0])
    return r.results[0]["out_0_dram"]
```
